# Optimizing a Trainium2 kernel written in Bass

```python
import numpy as np
import jax
import jax.numpy as jnp

def _softmax(x, axis=-1):
    return jax.nn.softmax(x, axis=axis)

def _gelu(x):
    return jax.nn.gelu(x, approximate=True)

def _silu(x):
    return jax.nn.silu(x)

def _sigmoid(x):
    return jax.nn.sigmoid(x)

def _layernorm(x, axis=-1, eps=1e-05):
    m = jnp.mean(x, axis=axis, keepdims=True)
    v = jnp.var(x, axis=axis, keepdims=True)
    return (x - m) / jnp.sqrt(v + eps)

def _scatter_add(tgt, idx, src, axis=0):
    return tgt.at[idx].add(src)

def _segment_sum(src, seg, n):
    return jax.ops.segment_sum(src, seg, n)
kernel_name = 'mk_prb_d1_jaxref_r8_0ee447'

def setup_inputs(seed: int=0):
    np.random.seed(seed)
    _w = jnp.asarray

    def _L0_attn_setup():
        import jax, jax.numpy as jnp
        import numpy as np
        B, S, HID = (2, 512, 512)
        H, HKV, D = (32, 8, 128)
        G = H // HKV
        EPS = 1e-06

        def _reference_tuple_inner(hidden_states, Wq, bq, Wk, bk, Wv, bv, Wo, M, z):
            b, s, _ = hidden_states.shape
            q = (hidden_states @ Wq.T + bq).reshape(b, s, H, D)
            k = (hidden_states @ Wk.T + bk).reshape(b, s, HKV, D)
            v = (hidden_states @ Wv.T + bv).reshape(b, s, HKV, D)
            sig_q = jax.nn.elu(q) + 1.0
            sig_k = jax.nn.elu(k) + 1.0
            q_sel = sig_q[:, :, ::G, :]
            num = jnp.einsum('bshd,hde->bshe', q_sel, M)
            den = jnp.einsum('bshd,hd->bsh', q_sel, z)[..., None] + EPS
            retrieved = num / den
            out_heads = jnp.repeat(retrieved, G, axis=2)
            output = out_heads.reshape(b, s, H * D) @ Wo.T
            M_new = M + jnp.einsum('bshd,bshe->hde', sig_k, v)
            z_new = z + sig_k.sum(axis=(0, 1))
            return (output, M_new, z_new)
        key = jax.random.key(seed)
        ks = jax.random.split(key, 10)
        s = 0.02
        return {'hidden_states': jax.random.normal(ks[0], (B, S, HID), jnp.float32), 'Wq': jax.random.normal(ks[1], (H * D, HID), jnp.float32) * s, 'bq': jnp.zeros((H * D,), jnp.float32), 'Wk': jax.random.normal(ks[2], (HKV * D, HID), jnp.float32) * s, 'bk': jnp.zeros((HKV * D,), jnp.float32), 'Wv': jax.random.normal(ks[3], (HKV * D, HID), jnp.float32) * s, 'bv': jnp.zeros((HKV * D,), jnp.float32), 'Wo': jax.random.normal(ks[4], (HID, H * D), jnp.float32) * s, 'M': jax.random.normal(ks[5], (HKV, D, D), jnp.float32), 'z': jax.random.uniform(ks[6], (HKV, D), jnp.float32) * 100.0 + 1.0}
    _L0_attn_in = _L0_attn_setup()

    def _L0_ffn_setup():
        import jax, jax.numpy as jnp
        import numpy as np
        B, S, D_IN, D_OUT = (4, 256, 512, 512)
        key = jax.random.key(seed)
        k1, k2, k3, k4 = jax.random.split(key, 4)
        inputs = jax.random.normal(k1, (B, S, D_IN), dtype=jnp.float32)
        w = jax.random.randint(k2, (D_IN, D_OUT), -128, 127, dtype=jnp.int8)
        w_scale = jax.random.uniform(k3, (D_IN, D_OUT), dtype=jnp.float32, minval=0.001, maxval=0.02)
        b = jax.random.normal(k4, (D_OUT,), dtype=jnp.float32)
        return {'inputs': inputs, 'w': w, 'w_scale': w_scale, 'b': b}
    _L0_ffn_in = _L0_ffn_setup()
    _d = {'L0_attn_hidden_states': _L0_attn_in['hidden_states'], 'L0_attn_Wq': _L0_attn_in['Wq'], 'L0_attn_bq': _L0_attn_in['bq'], 'L0_attn_Wk': _L0_attn_in['Wk'], 'L0_attn_bk': _L0_attn_in['bk'], 'L0_attn_Wv': _L0_attn_in['Wv'], 'L0_attn_bv': _L0_attn_in['bv'], 'L0_attn_Wo': _L0_attn_in['Wo'], 'L0_attn_M': _L0_attn_in['M'], 'L0_attn_z': _L0_attn_in['z'], 'L0_ffn_w': _L0_ffn_in['w'], 'L0_ffn_w_scale': _L0_ffn_in['w_scale'], 'L0_ffn_b': _L0_ffn_in['b']}
    _x0 = _d['L0_attn_hidden_states']
    _d['L0_attn_hidden_states'] = jax.random.normal(jax.random.fold_in(jax.random.key(seed), 1), (8, 256, 512), dtype=_x0.dtype)
    del _x0
    return _d

def reference(L0_attn_hidden_states, L0_attn_Wq, L0_attn_bq, L0_attn_Wk, L0_attn_bk, L0_attn_Wv, L0_attn_bv, L0_attn_Wo, L0_attn_M, L0_attn_z, L0_ffn_w, L0_ffn_w_scale, L0_ffn_b):

    def _L0_attn_ref(hidden_states, Wq, bq, Wk, bk, Wv, bv, Wo, M, z):
        import jax, jax.numpy as jnp
        import numpy as np
        B, S, HID = (2, 512, 512)
        H, HKV, D = (32, 8, 128)
        G = H // HKV
        EPS = 1e-06

        def _reference_tuple_inner(hidden_states, Wq, bq, Wk, bk, Wv, bv, Wo, M, z):
            b, s, _ = hidden_states.shape
            q = (hidden_states @ Wq.T + bq).reshape(b, s, H, D)
            k = (hidden_states @ Wk.T + bk).reshape(b, s, HKV, D)
            v = (hidden_states @ Wv.T + bv).reshape(b, s, HKV, D)
            sig_q = jax.nn.elu(q) + 1.0
            sig_k = jax.nn.elu(k) + 1.0
            q_sel = sig_q[:, :, ::G, :]
            num = jnp.einsum('bshd,hde->bshe', q_sel, M)
            den = jnp.einsum('bshd,hd->bsh', q_sel, z)[..., None] + EPS
            retrieved = num / den
            out_heads = jnp.repeat(retrieved, G, axis=2)
            output = out_heads.reshape(b, s, H * D) @ Wo.T
            M_new = M + jnp.einsum('bshd,bshe->hde', sig_k, v)
            z_new = z + sig_k.sum(axis=(0, 1))
            return (output, M_new, z_new)
        return _reference_tuple_inner(hidden_states, Wq, bq, Wk, bk, Wv, bv, Wo, M, z)[0]

    def _L0_ffn_ref(inputs, w, w_scale, b):
        import jax, jax.numpy as jnp
        import numpy as np
        B, S, D_IN, D_OUT = (4, 256, 512, 512)
        w_deq = w.astype(jnp.float32) * w_scale
        out = jnp.einsum('bsd,df->bsf', inputs, w_deq)
        return out + b
    x = L0_attn_hidden_states
    xn = _layernorm(x, axis=-1)
    x = x + _L0_attn_ref(xn, L0_attn_Wq, L0_attn_bq, L0_attn_Wk, L0_attn_bk, L0_attn_Wv, L0_attn_bv, L0_attn_Wo, L0_attn_M, L0_attn_z) + _L0_ffn_ref(xn, L0_ffn_w, L0_ffn_w_scale, L0_ffn_b)
    return x

_drawn_inputs = setup_inputs


def setup_inputs(seed=0):
    import zlib

    import numpy as np

    out = dict(_drawn_inputs(seed))
    spreads = {'L0_attn_bq': (0.0, 2.0), 'L0_attn_bk': (0.0, 0.1), 'L0_attn_bv': (0.0, 0.1)}
    factors = {'L0_attn_Wq': 200.0, 'L0_attn_Wo': 200.0, 'L0_attn_M': 200.0, 'L0_attn_z': 200.0}
    for name, (base, spread) in spreads.items():
        noise = np.random.default_rng([zlib.crc32(name.encode()), seed]).standard_normal(out[name].shape)
        drawn = base * np.exp(spread * noise) if base else spread * noise
        out[name] = jnp.asarray(drawn.astype(out[name].dtype))
    for name, factor in factors.items():
        out[name] = (out[name] * factor).astype(out[name].dtype)
    return out
```

```python
from contextlib import ExitStack

import concourse.bass as bass
from concourse import mybir

F32 = mybir.dt.float32
F32R = mybir.dt.float32r
I8 = mybir.dt.int8
I32 = mybir.dt.int32
ALU = mybir.AluOpType
ACT = mybir.ActivationFunctionType
AX = mybir.AxisListType

LN_EPS = 1e-5
DEN_EPS = 1e-6


def retrieval_and_dense(nc, x_d, Wq_d, bq_d, Wo_d, M_d, z_d, w_d, wscale_d, b_d, out_d):
    P = 128
    HID = x_d.shape[-1]
    G, D, _ = M_d.shape
    R = Wq_d.shape[0] // (G * D)
    K = HID // P
    E = G * D
    HALF = E // 2
    GH = G // 2
    NC = HID // P
    xr = x_d.rearrange("b s c -> (b s) c")
    T = xr.shape[0] // P
    AHEAD = 4
    LAG = 2
    SLOTS = 5
    PAIRS = (T - 2 - AHEAD) // 2
    EARLY = T - 2 * SLOTS
    assert P == D and HID == 512 and HALF == 512 and R == 4 and T == 16 and AHEAD < EARLY

    x_t = xr.rearrange("(t p) c -> t p c", p=P)
    out_t = out_d.rearrange("b s c -> (b s) c").rearrange("(t p) c -> t p c", p=P)
    wq_t = Wq_d.rearrange("(g r p) c -> p g r c", r=R, p=P)
    bq_g = bq_d.rearrange("(g r d) -> g r d", r=R, d=D)[:, 0, :]

    with ExitStack() as ctx:
        def sb(name, shape, dt=F32):
            return ctx.enter_context(nc.sbuf_tensor(name, shape, dt))

        def bank(name):
            return ctx.enter_context(nc.psum_tensor(name, [P, 512], F32))

        def sem(name):
            return ctx.enter_context(nc.semaphore(name))

        x = sb("x", [P, T, HID])
        xn = sb("xn", [P, HID])
        xT_hi = sb("xT_hi", [P, 2, K, P], F32R)
        xT_lo = sb("xT_lo", [P, 2, K, P], F32R)
        WqT_hi = sb("WqT_hi", [P, K, E], F32R)
        WqT_lo = sb("WqT_lo", [P, K, E], F32R)
        wd_hi = sb("wd_hi", [P, K, HID], F32R)
        wd_lo = sb("wd_lo", [P, K, HID], F32R)
        P_hi = sb("P_hi", [P, G, HID], F32R)
        P_lo = sb("P_lo", [P, G, HID], F32R)
        bq_b = sb("bq_b", [P, G, D])
        z_b = sb("z_b", [P, G, D])
        b_b = sb("b_b", [P, HID])
        tbuf = sb("tbuf", [P, 2, E])
        ebuf = sb("ebuf", [P, 2, E])
        a = sb("a", [P, 4, E])
        aT_hi = sb("aT_hi", [P, 2, G, P], F32R)
        aT_lo = sb("aT_lo", [P, 2, G, P], F32R)
        Wo_sum = sb("Wo_sum", [P, 2, G, D])
        WoT = sb("WoT", [P, 2, G, P])
        MT = sb("MT", [P, G, D])
        w_words = sb("w_words", [P, K, HID // 4], I32)
        w_i8 = w_words[:].bitcast(I8)
        ident = sb("ident", [P, P])
        neg_half = sb("neg_half", [P, 1])
        stats = sb("stats", [P, 6])
        meanvar = sb("meanvar", [P, 2, 2])
        vareps = sb("vareps", [P, 2, 1])
        rstd = sb("rstd", [P, 2, 1])
        den = sb("den", [P, G])
        den_e = sb("den_e", [P, G])
        rden = sb("rden", [P, G])

        def stage(slot):
            return x[:, EARLY + 2 * slot:EARLY + 2 * slot + 2, :].rearrange("p t c -> p (t c)")

        wscale = a[:, 0:2, :].rearrange("p s (k n) -> p (s k) n", n=HID)
        M_sb = a[:, 3, :].rearrange("p (g e) -> p g e", g=G)

        def a_slot(t, parity):
            return 2 + parity if isinstance(t, int) and t < LAG else parity

        xT_ps = bank("xT_ps")
        q_ps = [bank("q0_ps"), bank("q1_ps")]
        dense_ps = bank("dense_ps")
        aT_ps = [bank("aT0_ps"), bank("aT1_ps")]
        spare_ps = bank("spare_ps")
        attn_ps = bank("attn_ps")
        setup_ps = [aT_ps[0], aT_ps[1], spare_ps, attn_ps]

        x_in = [sem(f"x_in{t}") for t in range(EARLY)]
        x_rest_in = sem("x_rest_in")
        stage_in = [sem(f"stage_in{s}") for s in range(SLOTS)]
        w_in, wscale_in, bq_in, z_in, b_in, M_in = (
            sem(n) for n in ("w_in", "wscale_in", "bq_in", "z_in", "b_in", "M_in"))
        consts_set = sem("consts_set")
        stats_set = sem("stats_set")
        meanvar_ready = sem("meanvar_ready")
        vareps_ready = sem("vareps_ready")
        rstd_ready = sem("rstd_ready")
        xn_ready = sem("xn_ready")
        xT_filled = sem("xT_filled")
        xT_hi_ready = sem("xT_hi_ready")
        xT_lo_ready = sem("xT_lo_ready")
        setup_filled = sem("setup_filled")
        setup_copied = sem("setup_copied")
        setup_lo_ready = sem("setup_lo_ready")
        wd_ready = sem("wd_ready")
        wd_hi_ready = sem("wd_hi_ready")
        wd_lo_ready = sem("wd_lo_ready")
        pool_pairs = sem("pool_pairs")
        pool_summed = sem("pool_summed")
        dve_pairs = sem("dve_pairs")
        dve_summed = sem("dve_summed")
        q_filled = sem("q_filled")
        q_biased = sem("q_biased")
        qneg_ready = sem("qneg_ready")
        exp_ready = sem("exp_ready")
        s_ready = sem("s_ready")
        sz_ready = sem("sz_ready")
        den_ready = sem("den_ready")
        den_e_ready = sem("den_e_ready")
        rden_ready = sem("rden_ready")
        a_ready = sem("a_ready")
        xb_ready = sem("xb_ready")
        dense_filled = sem("dense_filled")
        dense_added = sem("dense_added")
        aT_filled = sem("aT_filled")
        aT_hi_ready = sem("aT_hi_ready")
        aT_lo_ready = sem("aT_lo_ready")
        attn_filled = sem("attn_filled")
        attn_added = sem("attn_added")
        stored = sem("stored")

        block = ctx.enter_context(nc.Block())

        WQ_USES = 2 * K
        M_USE = WQ_USES

        def wo_use(c):
            return M_USE + 2 + 4 * c

        USES = wo_use(NC)

        def lo_uses_before(u):
            return sum(1 for v in range(u) if v < WQ_USES or (v >= wo_use(0) and (v - wo_use(0)) % 4 >= 2))

        def has_lo(u):
            return lo_uses_before(u + 1) > lo_uses_before(u)

        def from_tile(t, n):
            return t >= n if isinstance(t, int) else True

        def tile(t):
            return x[:, bass.ds(t, 1), :].rearrange("p a c -> p (a c)")

        def wait_x(eng, t, parity):
            if isinstance(t, int) and t < EARLY:
                eng.wait_ge(x_in[t], 16)
            else:
                eng.wait_ge(x_rest_in, 8 * (t - parity) - 8 * EARLY + 16)

        @block.sync
        def _(sp):
            def load_x(t):
                sp.dma_start(x[:, t, :], x_t[t]).then_inc(x_in[t], 16)

            def load_wq(i):
                sp.dma_start(stage(i).rearrange("p (g c) -> p g c", g=2),
                             wq_t[:, 2 * i:2 * i + 2, 0, :]).then_inc(stage_in[i], 16)

            def load_wo(k):
                n = k + 4
                c, q = k // 4, k % 4
                if n - SLOTS >= 4:
                    old = n - SLOTS - 4
                    sp.wait_ge(pool_summed if old % 2 == 0 else dve_summed, old // 2 + 1)
                elif n >= SLOTS:
                    sp.wait_ge(setup_filled, ((n - SLOTS) // 2 + 1) * K)
                sp.dma_start(stage(n % SLOTS),
                             Wo_d[c * P:(c + 1) * P, q * 2 * R * D:(q + 1) * 2 * R * D]
                             ).then_inc(stage_in[n % SLOTS], 16)

            load_x(0)
            for i in range(4):
                load_wq(i)
            load_x(1)
            sp.dma_start(w_words[:], w_d.rearrange("(k p) n -> p k n", p=P)).then_inc(w_in, 16)
            sp.dma_start(wscale, wscale_d.rearrange("(k p) n -> p k n", p=P)).then_inc(wscale_in, 16)
            sp.dma_start(bq_b[:], bq_g.unsqueeze(0).to_broadcast([P, G, D])).then_inc(bq_in, 16)
            load_x(2)
            sp.dma_start(z_b[:], z_d.unsqueeze(0).to_broadcast([P, G, D])).then_inc(z_in, 16)
            sp.dma_start(M_sb, M_d.rearrange("g d e -> d g e")).then_inc(M_in, 16)
            sp.dma_start(b_b[:], b_d.unsqueeze(0).to_broadcast([P, HID])).then_inc(b_in, 16)
            load_x(3)
            for k in range(4 * NC):
                load_wo(k)
                if k == 5:
                    load_x(4)
                if k == 9:
                    load_x(5)
            for s in range(SLOTS):
                last = 4 * NC - SLOTS + s
                slot = (last + 4) % SLOTS
                assert slot == s
                sp.wait_ge(pool_summed if last % 2 == 0 else dve_summed, last // 2 + 1)
                t = EARLY + 2 * s
                sp.dma_start(x[:, t:t + 2, :], x_t[t:t + 2].rearrange("t p c -> p t c")
                             ).then_inc(x_rest_in, 16)
                sp.wait_ge(x_rest_in, 16 * (s + 1))
            with sp.Fori(0, T) as t:
                sp.wait_ge(attn_added, t + 1)
                sp.dma_start(out_t[bass.ds(t, 1)].rearrange("t p c -> p (t c)"), tile(t)).then_inc(stored, 16)
            sp.wait_ge(stored, 16 * T)

        @block.gpsimd
        def _(pool):
            def rstd_of(t, parity):
                pool.wait_ge(vareps_ready, t + 1)
                if from_tile(t, 2):
                    pool.wait_ge(xn_ready, t - 1)
                nc.gpsimd.tensor_tensor(rstd[:, parity, :], vareps[:, parity, :], neg_half[:], ALU.pow
                                        ).then_inc(rstd_ready, 1)

            def add_b(t):
                if isinstance(t, int) and t == 0:
                    pool.wait_ge(b_in, 16)
                pool.wait_ge(xn_ready, t + 1)
                nc.gpsimd.tensor_tensor(tile(t), tile(t), b_b[:], ALU.add).then_inc(xb_ready, 1)

            def times_z(t, parity, h):
                cols = slice(h * HALF, (h + 1) * HALF)
                if isinstance(t, int) and t == 0 and h == 0:
                    pool.wait_ge(z_in, 16)
                pool.wait_ge(s_ready, 2 * t + h + 1)
                nc.gpsimd.tensor_tensor(ebuf[:, parity, cols], tbuf[:, parity, cols],
                                        z_b[:].rearrange("p g d -> p (g d)")[:, cols], ALU.mult
                                        ).then_inc(sz_ready, 1)

            def sum_wo(c):
                for q in (0, 2):
                    k = 4 * c + q
                    n = k + 4
                    v = stage(n % SLOTS).rearrange("p (g u v d) -> p g u v d", g=2, u=2, v=2)
                    if c >= 2 and q == 0:
                        pool.wait_ge(setup_filled, wo_use(c - 2) + 2)
                    pool.wait_ge(stage_in[n % SLOTS], 16 * (n // SLOTS + 1))
                    nc.gpsimd.tensor_tensor(v[:, :, :, 0, :], v[:, :, :, 0, :], v[:, :, :, 1, :], ALU.add
                                            ).then_inc(pool_pairs, 1)
                    pool.wait_ge(pool_pairs, k // 2 + 1)
                    nc.gpsimd.tensor_tensor(Wo_sum[:, c % 2, 2 * q:2 * q + 2, :], v[:, :, 0, 0, :],
                                            v[:, :, 1, 0, :], ALU.add).then_inc(pool_summed, 1)

            nc.gpsimd.memset(neg_half[:], -0.5).then_inc(consts_set, 1)
            nc.gpsimd.memset(ident[:], 0.0).then_inc(consts_set, 1)
            pool.wait_ge(consts_set, 2)
            nc.gpsimd.affine_select(out=ident[:], in_=ident[:], compare_op=ALU.not_equal, fill=1.0,
                                    base=0, pattern=[[-1, P]], channel_multiplier=1).then_inc(consts_set, 1)
            rstd_of(0, 0)
            rstd_of(1, 1)

            def q_step(t, parity, stats_ahead=True):
                if stats_ahead:
                    rstd_of(t + 2, parity)
                add_b(t)
                for h in range(2):
                    times_z(t, parity, h)

            for t in range(AHEAD):
                q_step(t, t % 2)
                sum_wo(t)
            with pool.Fori(0, PAIRS) as i:
                t = AHEAD + 2 * i
                for j in range(2):
                    q_step(t + j, j)
            for t in range(T - 2, T):
                q_step(t, t % 2, stats_ahead=False)

        @block.scalar
        def _(act):
            def copy_xT_hi(t, parity):
                act.wait_ge(xT_filled, t + 1)
                if from_tile(t, 2):
                    act.wait_ge(dense_filled, t - 1)
                nc.scalar.activation(xT_hi[:, parity, :, :].rearrange("p k r -> p (k r)"), xT_ps[:], ACT.Copy
                                     ).then_inc(xT_hi_ready, 1)

            def exp_of(t, parity, h):
                cols = slice(h * HALF, (h + 1) * HALF)
                act.wait_ge(q_biased, 2 * t + h + 1)
                if from_tile(t, 2):
                    act.wait_ge(den_ready, t - 1)
                nc.scalar.activation(ebuf[:, parity, cols], tbuf[:, parity, cols], ACT.Relu, scale=-1.0
                                     ).then_inc(qneg_ready, 1)
                act.wait_ge(qneg_ready, 2 * t + h + 1)
                nc.scalar.activation(ebuf[:, parity, cols], ebuf[:, parity, cols], ACT.Exp, scale=-1.0
                                     ).then_inc(exp_ready, 1)

            def copy_aT_hi(t, parity, h):
                act.wait_ge(aT_filled, 2 * t + h + 1)
                if from_tile(t, 2):
                    act.wait_ge(attn_filled, t - 1)
                nc.scalar.activation(aT_hi[:, parity, h * GH:(h + 1) * GH, :].rearrange("p g r -> p (g r)"),
                                     aT_ps[h][:], ACT.Copy).then_inc(aT_hi_ready, 1)

            def copy_setup(u, out):
                act.wait_ge(setup_filled, u + 1)
                nc.scalar.activation(out, setup_ps[u % 4][:].rearrange("p (g c) -> p g c", g=4), ACT.Copy
                                     ).then_inc(setup_copied, 1)

            copy_xT_hi(0, 0)
            for u in range(WQ_USES):
                h, k = u // K, u % K
                copy_setup(u, WqT_hi[:, k, h * HALF:(h + 1) * HALF].rearrange("p (g c) -> p g c", g=4))

            def q_step(t, parity, next_x=True):
                if next_x:
                    copy_xT_hi(t + 1, 1 - parity)
                for h in range(2):
                    exp_of(t, parity, h)

            for t in range(AHEAD):
                copy_xT_hi(t + 1, (t + 1) % 2)
                if t == 0:
                    for j in range(2):
                        ks = slice(j * K // 2, (j + 1) * K // 2)
                        act.wait_ge(wd_ready, j + 1)
                        nc.scalar.activation(wd_hi[:, ks, :], wscale[:, ks, :], ACT.Copy).then_inc(wd_hi_ready, 1)
                exp_of(t, t % 2, 0)
                if t > 0:
                    c = t - 1
                    if c >= 2:
                        act.wait_ge(setup_filled, wo_use(c - 2) + 4)
                    for h in range(2):
                        copy_setup(wo_use(c) + h, WoT[:, c % 2, h * GH:(h + 1) * GH, :])
                exp_of(t, t % 2, 1)
                if t == 0:
                    for h in range(2):
                        copy_setup(M_USE + h, MT[:, h * GH:(h + 1) * GH, :])
                else:
                    for h in range(2):
                        copy_setup(wo_use(c) + 2 + h, P_hi[:, h * GH:(h + 1) * GH, c * P:(c + 1) * P])
            c = NC - 1
            act.wait_ge(setup_filled, wo_use(c - 2) + 4)
            for h in range(2):
                copy_setup(wo_use(c) + h, WoT[:, c % 2, h * GH:(h + 1) * GH, :])
            for h in range(2):
                copy_setup(wo_use(c) + 2 + h, P_hi[:, h * GH:(h + 1) * GH, c * P:(c + 1) * P])

            def o_step(t, parity):
                for h in range(2):
                    copy_aT_hi(t, parity, h)

            for t in range(LAG):
                o_step(t, t % 2)
            with act.Fori(0, PAIRS) as i:
                t = AHEAD + 2 * i
                for j in range(2):
                    o_step(t + j - LAG, j)
                    q_step(t + j, j)
            for t in range(T - 2, T):
                o_step(t - LAG, t % 2)
                q_step(t, t % 2, next_x=t + 1 < T)
            for t in range(T - LAG, T):
                o_step(t, t % 2)

        @block.vector
        def _(dve):
            def statistics(t, parity):
                wait_x(dve, t, parity)
                nc.vector.bn_stats(stats[:], tile(t)).then_inc(stats_set, 1)

            def mean_and_variance(t, parity):
                nc.vector.bn_aggr(meanvar[:, parity, :], stats[:]).then_inc(meanvar_ready, 1)

            def variance_eps(t, parity):
                dve.wait_ge(meanvar_ready, t + 1)
                if from_tile(t, 2):
                    dve.wait_ge(rstd_ready, t - 1)
                nc.vector.tensor_scalar_add(vareps[:, parity, :], meanvar[:, parity, 1:2], LN_EPS
                                            ).then_inc(vareps_ready, 1)

            def normalise(t, parity):
                dve.wait_ge(rstd_ready, t + 1)
                if from_tile(t, 1):
                    dve.wait_ge(xT_filled, t)
                nc.vector.tensor_scalar(xn[:], tile(t), meanvar[:, parity, 0:1], rstd[:, parity, :],
                                        ALU.subtract, ALU.mult).then_inc(xn_ready, 1)

            def split_xT_lo(t, parity):
                dve.wait_ge(xT_hi_ready, t + 1)
                if from_tile(t, 2):
                    dve.wait_ge(dense_filled, t - 1)
                nc.vector.tensor_tensor(xT_lo[:, parity, :, :].rearrange("p k r -> p (k r)"), xT_ps[:],
                                        xT_hi[:, parity, :, :].rearrange("p k r -> p (k r)").bitcast(F32),
                                        ALU.subtract).then_inc(xT_lo_ready, 1)

            def setup_lo(u, out, hi):
                dve.wait_ge(setup_copied, u + 1)
                nc.vector.tensor_tensor(out, setup_ps[u % 4][:].rearrange("p (g c) -> p g c", g=4),
                                        hi.bitcast(F32), ALU.subtract).then_inc(setup_lo_ready, 1)

            def add_bias(t, parity, h):
                cols = slice(h * HALF, (h + 1) * HALF)
                if isinstance(t, int) and t == 0 and h == 0:
                    dve.wait_ge(bq_in, 16)
                dve.wait_ge(q_filled, 2 * t + h + 1)
                nc.vector.tensor_tensor(tbuf[:, parity, cols], q_ps[h][:],
                                        bq_b[:].rearrange("p g d -> p (g d)")[:, cols], ALU.add
                                        ).then_inc(q_biased, 1)

            def make_s(t, parity, h):
                cols = slice(h * HALF, (h + 1) * HALF)
                dve.wait_ge(exp_ready, 2 * t + h + 1)
                nc.vector.scalar_tensor_tensor(tbuf[:, parity, cols], tbuf[:, parity, cols], 0.0,
                                               ebuf[:, parity, cols], ALU.max, ALU.add).then_inc(s_ready, 1)

            def denominator(t, parity):
                dve.wait_ge(sz_ready, 2 * t + 2)
                nc.vector.reduce_sum(den[:], ebuf[:, parity, :].rearrange("p (g d) -> p g d", g=G), AX.X
                                     ).then_inc(den_ready, 1)
                dve.wait_ge(den_ready, t + 1)
                nc.vector.tensor_scalar_add(den_e[:], den[:], DEN_EPS).then_inc(den_e_ready, 1)
                dve.wait_ge(den_e_ready, t + 1)
                nc.vector.reciprocal(rden[:], den_e[:]).then_inc(rden_ready, 1)

            def make_a(t, parity):
                if isinstance(t, int) and t == 1:
                    dve.wait_ge(setup_filled, M_USE + 2)
                if isinstance(t, int) and t in (2, 3):
                    dve.wait_ge(wd_hi_ready, 2)
                if from_tile(t, 4):
                    dve.wait_ge(aT_filled, 2 * t - 2)
                dve.wait_ge(rden_ready, t + 1)
                nc.vector.tensor_tensor(a[:, a_slot(t, parity), :].rearrange("p (g d) -> p g d", g=G),
                                        tbuf[:, parity, :].rearrange("p (g d) -> p g d", g=G),
                                        rden[:].unsqueeze(2).to_broadcast([P, G, D]), ALU.mult
                                        ).then_inc(a_ready, 1)

            def add_dense(t):
                dve.wait_ge(dense_filled, t + 1)
                dve.wait_ge(xb_ready, t + 1)
                nc.vector.tensor_tensor(tile(t), dense_ps[:], tile(t), ALU.add).then_inc(dense_added, 1)

            def split_aT_lo(t, parity, h):
                gs = slice(h * GH, (h + 1) * GH)
                dve.wait_ge(aT_hi_ready, 2 * t + h + 1)
                if from_tile(t, 2):
                    dve.wait_ge(attn_filled, t - 1)
                nc.vector.tensor_tensor(aT_lo[:, parity, gs, :].rearrange("p g r -> p (g r)"), aT_ps[h][:],
                                        aT_hi[:, parity, gs, :].rearrange("p g r -> p (g r)").bitcast(F32),
                                        ALU.subtract).then_inc(aT_lo_ready, 1)

            def add_attn(t):
                dve.wait_ge(attn_filled, t + 1)
                dve.wait_ge(dense_added, t + 1)
                nc.vector.tensor_tensor(tile(t), attn_ps[:], tile(t), ALU.add).then_inc(attn_added, 1)

            def sum_wo(c):
                for q in (1, 3):
                    k = 4 * c + q
                    n = k + 4
                    v = stage(n % SLOTS).rearrange("p (g u v d) -> p g u v d", g=2, u=2, v=2)
                    if c >= 2 and q == 1:
                        dve.wait_ge(setup_filled, wo_use(c - 2) + 2)
                    dve.wait_ge(stage_in[n % SLOTS], 16 * (n // SLOTS + 1))
                    nc.vector.tensor_tensor(v[:, :, :, 0, :], v[:, :, :, 0, :], v[:, :, :, 1, :], ALU.add
                                            ).then_inc(dve_pairs, 1)
                    dve.wait_ge(dve_pairs, k // 2 + 1)
                    nc.vector.tensor_tensor(Wo_sum[:, c % 2, 2 * q:2 * q + 2, :], v[:, :, 0, 0, :],
                                            v[:, :, 1, 0, :], ALU.add).then_inc(dve_summed, 1)

            def P_split(c):
                for h in range(2):
                    gs, ns = slice(h * GH, (h + 1) * GH), slice(c * P, (c + 1) * P)
                    setup_lo(wo_use(c) + 2 + h, P_lo[:, gs, ns], P_hi[:, gs, ns])

            for t in range(2):
                statistics(t, t)
                dve.wait_ge(stats_set, t + 1)
                mean_and_variance(t, t)
                variance_eps(t, t)
            normalise(0, 0)
            split_xT_lo(0, 0)
            normalise(1, 1)
            for u in range(WQ_USES):
                h, k = u // K, u % K
                cs = slice(h * HALF, (h + 1) * HALF)
                setup_lo(u, WqT_lo[:, k, cs].rearrange("p (g c) -> p g c", g=4),
                         WqT_hi[:, k, cs].rearrange("p (g c) -> p g c", g=4))
            dve.wait_ge(w_in, 16)
            dve.wait_ge(wscale_in, 16)
            for j in range(2):
                ks = slice(j * K // 2, (j + 1) * K // 2)
                nc.vector.tensor_tensor(wscale[:, ks, :], w_i8[:, ks, :], wscale[:, ks, :], ALU.mult
                                        ).then_inc(wd_ready, 1)

            def q_step(t, parity, stats_ahead=True, next_x=True):
                if stats_ahead:
                    statistics(t + 2, parity)
                    dve.wait_ge(stats_set, t + 3)
                add_bias(t, parity, 0)
                if stats_ahead:
                    mean_and_variance(t + 2, parity)
                    variance_eps(t + 2, parity)
                if next_x:
                    split_xT_lo(t + 1, 1 - parity)
                if isinstance(t, int) and t == 0:
                    for j in range(2):
                        ks = slice(j * K // 2, (j + 1) * K // 2)
                        dve.wait_ge(wd_hi_ready, j + 1)
                        nc.vector.tensor_tensor(wd_lo[:, ks, :], wscale[:, ks, :], wd_hi[:, ks, :].bitcast(F32),
                                                ALU.subtract).then_inc(wd_lo_ready, 1)
                if from_tile(t, 1):
                    denominator(t - 1, 1 - parity)
                add_bias(t, parity, 1)
                if from_tile(t, 1):
                    make_a(t - 1, 1 - parity)
                if stats_ahead:
                    normalise(t + 2, parity)
                for h in range(2):
                    make_s(t, parity, h)
                add_dense(t)

            def o_start(t, parity):
                for h in range(2):
                    split_aT_lo(t, parity, h)

            for t in range(AHEAD):
                q_step(t, t % 2)
                sum_wo(t)
                if t > 0:
                    P_split(t - 1)
            P_split(NC - 1)
            for t in range(LAG):
                o_start(t, t % 2)
                add_attn(t)
            with dve.Fori(0, PAIRS) as i:
                t = AHEAD + 2 * i
                for j in range(2):
                    o_start(t + j - LAG, j)
                    q_step(t + j, j)
                    add_attn(t + j - LAG)
            for t in range(T - 2, T):
                o_start(t - LAG, t % 2)
                q_step(t, t % 2, stats_ahead=False, next_x=t + 1 < T)
                add_attn(t - LAG)
            denominator(T - 1, (T - 1) % 2)
            make_a(T - 1, (T - 1) % 2)
            for t in range(T - LAG, T):
                o_start(t, t % 2)
                add_attn(t)

        @block.tensor
        def _(pe):
            def transpose_x(t):
                if isinstance(t, int) and t == 0:
                    pe.wait_ge(consts_set, 3)
                pe.wait_ge(xn_ready, t + 1)
                if from_tile(t, 1):
                    pe.wait_ge(xT_lo_ready, t)
                for k in range(K):
                    last = nc.tensor.transpose(xT_ps[:, k * P:(k + 1) * P], xn[:, k * P:(k + 1) * P], ident[:])
                last.then_inc(xT_filled, 1)

            def three_passes(out, xs, ws):
                n = len(xs)
                for i, ((x_hi, x_lo), (w_hi, w_lo)) in enumerate(zip(xs, ws)):
                    nc.tensor.matmul(out, x_hi, w_hi, start=(i == 0), stop=False)
                    nc.tensor.matmul(out, x_hi, w_lo, start=False, stop=False)
                    last = nc.tensor.matmul(out, x_lo, w_hi, start=False, stop=(i == n - 1))
                return last

            def xT_parts(parity):
                return [(xT_hi[:, parity, k, :], xT_lo[:, parity, k, :]) for k in range(K)]

            def product_q(t, parity, h):
                cols = slice(h * HALF, (h + 1) * HALF)
                pe.wait_ge(xT_lo_ready, t + 1)
                if isinstance(t, int) and t == 0:
                    pe.wait_ge(setup_lo_ready, (h + 1) * K)
                if from_tile(t, 1):
                    pe.wait_ge(q_biased, 2 * t - 1 + h)
                three_passes(q_ps[h][:], xT_parts(parity),
                             [(WqT_hi[:, k, cols], WqT_lo[:, k, cols]) for k in range(K)]).then_inc(q_filled, 1)

            def product_dense(t, parity):
                if isinstance(t, int) and t == 0:
                    pe.wait_ge(wd_lo_ready, 2)
                if from_tile(t, 1):
                    pe.wait_ge(dense_added, t)
                three_passes(dense_ps[:], xT_parts(parity),
                             [(wd_hi[:, k, :], wd_lo[:, k, :]) for k in range(K)]).then_inc(dense_filled, 1)

            def transpose_a(t, parity):
                pe.wait_ge(a_ready, t + 1)
                for h in range(2):
                    if from_tile(t, 1):
                        pe.wait_ge(aT_lo_ready, 2 * t - 1 + h)
                    for i in range(GH):
                        g = h * GH + i
                        last = nc.tensor.transpose(aT_ps[h][:, i * P:(i + 1) * P],
                                                   a[:, a_slot(t, parity), g * D:(g + 1) * D], ident[:])
                    last.then_inc(aT_filled, 1)

            def product_attn(t, parity):
                pe.wait_ge(aT_lo_ready, 2 * t + 2)
                if from_tile(t, 1):
                    pe.wait_ge(attn_added, t)
                three_passes(attn_ps[:], [(aT_hi[:, parity, g, :], aT_lo[:, parity, g, :]) for g in range(G)],
                             [(P_hi[:, g, :], P_lo[:, g, :]) for g in range(G)]).then_inc(attn_filled, 1)

            def setup_free(u):
                if u >= 4:
                    if has_lo(u - 4):
                        pe.wait_ge(setup_lo_ready, lo_uses_before(u - 4) + 1)
                    else:
                        pe.wait_ge(setup_copied, u - 3)

            def transposes(u, blocks):
                setup_free(u)
                for i, block_in in enumerate(blocks):
                    last = nc.tensor.transpose(setup_ps[u % 4][:, i * P:(i + 1) * P], block_in, ident[:])
                last.then_inc(setup_filled, 1)

            def transpose_wq():
                for u in range(WQ_USES):
                    h, k = u // K, u % K
                    if k == 0:
                        for i in (2 * h, 2 * h + 1):
                            pe.wait_ge(stage_in[i], 16)
                    transposes(u, [stage(2 * h + i // 2)[:, (i % 2) * HID + k * P:(i % 2) * HID + (k + 1) * P]
                                   for i in range(GH)])

            def transpose_m():
                pe.wait_ge(M_in, 16)
                for h in range(2):
                    transposes(M_USE + h, [M_sb[:, h * GH + i, :] for i in range(GH)])

            def transpose_wo(c):
                pe.wait_ge(pool_summed, 2 * c + 2)
                pe.wait_ge(dve_summed, 2 * c + 2)
                for h in range(2):
                    transposes(wo_use(c) + h, [Wo_sum[:, c % 2, h * GH + i, :] for i in range(GH)])

            def product_P(c):
                for h in range(2):
                    u = wo_use(c) + 2 + h
                    pe.wait_ge(setup_copied, wo_use(c) + h + 1)
                    setup_free(u)
                    for i in range(GH):
                        g = h * GH + i
                        last = nc.tensor.matmul(setup_ps[u % 4][:, i * P:(i + 1) * P], MT[:, g, :],
                                                WoT[:, c % 2, g, :], start=True, stop=True)
                    last.then_inc(setup_filled, 1)

            transpose_x(0)
            transpose_wq()
            for t in range(AHEAD):
                product_q(t, t % 2, 0)
                transpose_x(t + 1)
                product_q(t, t % 2, 1)
                if t > 0:
                    transpose_wo(t - 1)
                product_dense(t, t % 2)
                if t == 0:
                    transpose_m()
                else:
                    product_P(t - 1)
            transpose_wo(NC - 1)
            product_P(NC - 1)

            pe.wait_ge(setup_lo_ready, lo_uses_before(USES))
            for t in range(LAG):
                transpose_a(t, t % 2)
                product_attn(t, t % 2)
            with pe.Fori(0, PAIRS) as i:
                t = AHEAD + 2 * i
                for j in range(2):
                    transpose_a(t + j - LAG, j)
                    product_q(t + j, j, 0)
                    transpose_x(t + j + 1)
                    product_q(t + j, j, 1)
                    product_dense(t + j, j)
                    product_attn(t + j - LAG, j)
            for t in range(T - 2, T):
                transpose_a(t - LAG, t % 2)
                product_q(t, t % 2, 0)
                if t + 1 < T:
                    transpose_x(t + 1)
                product_q(t, t % 2, 1)
                product_dense(t, t % 2)
                product_attn(t - LAG, t % 2)
            for t in range(T - LAG, T):
                transpose_a(t, t % 2)
                product_attn(t, t % 2)


_INS = ["L0_attn_hidden_states", "L0_attn_Wq", "L0_attn_bq", "L0_attn_Wo", "L0_attn_M", "L0_attn_z",
        "L0_ffn_w", "L0_ffn_w_scale", "L0_ffn_b"]


def kernel(**inputs):
    import numpy as np
    import concourse.bacc as bacc
    from concourse.bass_utils import run_bass_kernel_spmd

    nc = bacc.Bacc("TRN2", target_bir_lowering=False, num_devices=1)
    arrays, args = {}, []
    for name in _INS:
        v = np.ascontiguousarray(inputs[name])
        if v.dtype == np.int8:
            v = v.view(np.int32)
        arrays[f"in_{name}"] = v
        args.append(nc.dram_tensor(f"in_{name}", v.shape, mybir.dt.from_np(v.dtype), kind="ExternalInput").ap())
    shape = inputs["L0_attn_hidden_states"].shape
    out = nc.dram_tensor("out", shape, F32, kind="ExternalOutput").ap()
    retrieval_and_dense(nc, *args, out)
    result = run_bass_kernel_spmd(nc, [arrays], core_ids=[0])
    return result.results[0]["out"]
```

```python
from contextlib import ExitStack

import concourse.bass as bass
from concourse import mybir

F32 = mybir.dt.float32
F32R = mybir.dt.float32r
I8 = mybir.dt.int8
I32 = mybir.dt.int32
ALU = mybir.AluOpType
ACT = mybir.ActivationFunctionType
AX = mybir.AxisListType

LN_EPS = 1e-5
DEN_EPS = 1e-6


def retrieval_and_dense(nc, x_d, Wq_d, bq_d, Wo_d, M_d, z_d, w_d, wscale_d, b_d, out_d):
    P = 128
    HID = x_d.shape[-1]
    G, D, _ = M_d.shape
    R = Wq_d.shape[0] // (G * D)
    K = HID // P
    E = G * D
    HALF = E // 2
    GH = G // 2
    NC = HID // P
    xr = x_d.rearrange("b s c -> (b s) c")
    T = xr.shape[0] // P
    AHEAD = 4
    LAG = 2
    SLOTS = 5
    PAIRS = (T - 2 - AHEAD) // 2
    EARLY = T - 2 * SLOTS
    assert P == D and HID == 512 and HALF == 512 and R == 4 and T == 16 and AHEAD < EARLY

    x_t = xr.rearrange("(t p) c -> t p c", p=P)
    out_t = out_d.rearrange("b s c -> (b s) c").rearrange("(t p) c -> t p c", p=P)
    wq_t = Wq_d.rearrange("(g r p) c -> p g r c", r=R, p=P)
    bq_g = bq_d.rearrange("(g r d) -> g r d", r=R, d=D)[:, 0, :]

    with ExitStack() as ctx:
        def sb(name, shape, dt=F32):
            return ctx.enter_context(nc.sbuf_tensor(name, shape, dt))

        def bank(name):
            return ctx.enter_context(nc.psum_tensor(name, [P, 512], F32))

        def sem(name):
            return ctx.enter_context(nc.semaphore(name))

        x = sb("x", [P, T, HID])
        xn = sb("xn", [P, HID])
        xT_hi = sb("xT_hi", [P, 2, K, P], F32R)
        xT_lo = sb("xT_lo", [P, 2, K, P], F32R)
        WqT_hi = sb("WqT_hi", [P, K, E], F32R)
        WqT_lo = sb("WqT_lo", [P, K, E], F32R)
        wd_hi = sb("wd_hi", [P, K, HID], F32R)
        wd_lo = sb("wd_lo", [P, K, HID], F32R)
        P_hi = sb("P_hi", [P, G, HID], F32R)
        P_lo = sb("P_lo", [P, G, HID], F32R)
        bq_b = sb("bq_b", [P, G, D])
        z_b = sb("z_b", [P, G, D])
        b_b = sb("b_b", [P, HID])
        tbuf = sb("tbuf", [P, 2, E])
        ebuf = sb("ebuf", [P, 2, E])
        a = sb("a", [P, 4, E])
        aT_hi = sb("aT_hi", [P, 2, G, P], F32R)
        aT_lo = sb("aT_lo", [P, 2, G, P], F32R)
        Wo_sum = sb("Wo_sum", [P, 2, G, D])
        WoT = sb("WoT", [P, 2, G, P])
        MT = sb("MT", [P, G, D])
        w_words = sb("w_words", [P, K, HID // 4], I32)
        w_i8 = w_words[:].bitcast(I8)
        ident = sb("ident", [P, P])
        neg_half = sb("neg_half", [P, 1])
        stats = sb("stats", [P, 6])
        meanvar = sb("meanvar", [P, 2, 2])
        vareps = sb("vareps", [P, 2, 1])
        rstd = sb("rstd", [P, 2, 1])
        den = sb("den", [P, G])
        den_e = sb("den_e", [P, G])
        rden = sb("rden", [P, 2, G])

        def stage(slot):
            return x[:, EARLY + 2 * slot:EARLY + 2 * slot + 2, :].rearrange("p t c -> p (t c)")

        wscale = a[:, 0:2, :].rearrange("p s (k n) -> p (s k) n", n=HID)
        w_f32 = Wo_sum[:].rearrange("p c g d -> p (c g d)").rearrange("p (k n) -> p k n", n=HID)
        M_sb = a[:, 3, :].rearrange("p (g e) -> p g e", g=G)

        def a_slot(t, parity):
            return 2 + parity if isinstance(t, int) and t < LAG else parity

        xT_ps = bank("xT_ps")
        q_ps = [bank("q0_ps"), bank("q1_ps")]
        dense_ps = bank("dense_ps")
        aT_ps = [bank("aT0_ps"), bank("aT1_ps")]
        spare_ps = bank("spare_ps")
        attn_ps = bank("attn_ps")

        x_in = [sem(f"x_in{t}") for t in range(EARLY)]
        x_rest_in = sem("x_rest_in")
        stage_in = [sem(f"stage_in{s}") for s in range(SLOTS)]
        w_in, wscale_in, bq_in, z_in, b_in, M_in = (
            sem(n) for n in ("w_in", "wscale_in", "bq_in", "z_in", "b_in", "M_in"))
        consts_set = sem("consts_set")
        stats_set = sem("stats_set")
        meanvar_ready = sem("meanvar_ready")
        vareps_ready = sem("vareps_ready")
        rstd_ready = sem("rstd_ready")
        xn_ready = sem("xn_ready")
        xT_filled = sem("xT_filled")
        xT_hi_ready = sem("xT_hi_ready")
        xT_lo_ready = sem("xT_lo_ready")
        setup_filled = sem("setup_filled")
        setup_copied = sem("setup_copied")
        setup_lo_ready = sem("setup_lo_ready")
        w_cast = sem("w_cast")
        wd_ready = sem("wd_ready")
        wd_hi_ready = sem("wd_hi_ready")
        wd_lo_ready = sem("wd_lo_ready")
        pool_pairs = sem("pool_pairs")
        pool_summed = sem("pool_summed")
        dve_pairs = sem("dve_pairs")
        dve_summed = sem("dve_summed")
        q_filled = sem("q_filled")
        q_biased = sem("q_biased")
        qneg_ready = sem("qneg_ready")
        exp_ready = sem("exp_ready")
        s_ready = sem("s_ready")
        sz_ready = sem("sz_ready")
        den_ready = sem("den_ready")
        den_e_ready = sem("den_e_ready")
        rden_ready = sem("rden_ready")
        a_ready = sem("a_ready")
        b_added = sem("b_added")
        dense_filled = sem("dense_filled")
        dense_added = sem("dense_added")
        aT_filled = sem("aT_filled")
        aT_hi_ready = sem("aT_hi_ready")
        aT_lo_ready = sem("aT_lo_ready")
        attn_filled = sem("attn_filled")
        attn_added = sem("attn_added")
        stored = sem("stored")

        block = ctx.enter_context(nc.Block())

        SETUP = [("wq", h, k) for h in range(2) for k in range(K)] + [("m", 0, h) for h in range(2)]
        SETUP += [(kind, c, h) for c in range(NC) for kind in ("wo", "p") for h in range(2)]
        USE = {what: u for u, what in enumerate(SETUP)}

        def setup_bank(what):
            kind, c, h = what
            if kind == "wq":
                return [aT_ps[0], aT_ps[1], spare_ps, attn_ps, dense_ps, q_ps[1], aT_ps[0], aT_ps[1]][USE[what]]
            if kind == "wo":
                return aT_ps[h]
            if what[:2] == ("p", NC - 1):
                return q_ps[1 - h]
            return [spare_ps, attn_ps][h]

        def filled_by(what):
            return USE[what] + 1

        def lo_by(what):
            return sum(1 for v in SETUP[:USE[what] + 1] if v[0] in ("wq", "p"))

        def from_tile(t, n):
            return t >= n if isinstance(t, int) else True

        def tile(t):
            return x[:, bass.ds(t, 1), :].rearrange("p a c -> p (a c)")

        def wait_x(eng, t, parity):
            if isinstance(t, int) and t < EARLY:
                eng.wait_ge(x_in[t], 16)
            else:
                eng.wait_ge(x_rest_in, 8 * (t - parity) - 8 * EARLY + 16)

        @block.sync
        def _(sp):
            def load_x(t):
                sp.dma_start(x[:, t, :], x_t[t]).then_inc(x_in[t], 16)

            def load_wq(i):
                sp.dma_start(stage(i).rearrange("p (g c) -> p g c", g=2),
                             wq_t[:, 2 * i:2 * i + 2, 0, :]).then_inc(stage_in[i], 16)

            def load_wo(k):
                n = k + 4
                c, q = k // 4, k % 4
                if n - SLOTS >= 4:
                    old = n - SLOTS - 4
                    sp.wait_ge(pool_summed if old % 2 == 0 else dve_summed, old // 2 + 1)
                elif n >= SLOTS:
                    sp.wait_ge(setup_filled, filled_by(("wq", (n - SLOTS) // 2, K - 1)))
                sp.dma_start(stage(n % SLOTS),
                             Wo_d[c * P:(c + 1) * P, q * 2 * R * D:(q + 1) * 2 * R * D]
                             ).then_inc(stage_in[n % SLOTS], 16)

            load_x(0)
            load_wq(0)
            load_wq(1)
            load_wq(2)
            load_wq(3)
            load_x(1)
            sp.dma_start(w_words[:], w_d.rearrange("(k p) n -> p k n", p=P)).then_inc(w_in, 16)
            sp.dma_start(bq_b[:], bq_g.unsqueeze(0).to_broadcast([P, G, D])).then_inc(bq_in, 16)
            sp.dma_start(wscale, wscale_d.rearrange("(k p) n -> p k n", p=P)).then_inc(wscale_in, 16)
            load_x(2)
            sp.dma_start(z_b[:], z_d.unsqueeze(0).to_broadcast([P, G, D])).then_inc(z_in, 16)
            sp.dma_start(b_b[:], b_d.unsqueeze(0).to_broadcast([P, HID])).then_inc(b_in, 16)
            sp.dma_start(M_sb, M_d.rearrange("g d e -> d g e")).then_inc(M_in, 16)
            load_x(3)
            for k in range(4 * NC):
                load_wo(k)
                if k == 4:
                    load_x(4)
                if k == 9:
                    load_x(5)
            for s in range(SLOTS):
                last = 4 * NC - SLOTS + s
                slot = (last + 4) % SLOTS
                assert slot == s
                sp.wait_ge(pool_summed if last % 2 == 0 else dve_summed, last // 2 + 1)
                t = EARLY + 2 * s
                sp.dma_start(x[:, t:t + 2, :], x_t[t:t + 2].rearrange("t p c -> p t c")
                             ).then_inc(x_rest_in, 16)
                sp.wait_ge(x_rest_in, 16 * (s + 1))
            with sp.Fori(0, T) as t:
                sp.wait_ge(attn_added, t + 1)
                sp.dma_start(out_t[bass.ds(t, 1)].rearrange("t p c -> p (t c)"), tile(t)).then_inc(stored, 16)
            sp.wait_ge(stored, 16 * T)

        @block.gpsimd
        def _(pool):
            def rstd_of(t, parity):
                pool.wait_ge(vareps_ready, t + 1)
                if from_tile(t, 2):
                    pool.wait_ge(xn_ready, t - 1)
                nc.gpsimd.tensor_tensor(rstd[:, parity, :], vareps[:, parity, :], neg_half[:], ALU.pow
                                        ).then_inc(rstd_ready, 1)

            def add_b(t):
                if isinstance(t, int) and t == 0:
                    pool.wait_ge(b_in, 16)
                pool.wait_ge(dense_added, t + 1)
                nc.gpsimd.tensor_tensor(tile(t), tile(t), b_b[:], ALU.add).then_inc(b_added, 1)

            def times_z(t, parity, h):
                cols = slice(h * HALF, (h + 1) * HALF)
                if isinstance(t, int) and t == 0 and h == 0:
                    pool.wait_ge(z_in, 16)
                pool.wait_ge(s_ready, 2 * t + h + 1)
                nc.gpsimd.tensor_tensor(ebuf[:, parity, cols], tbuf[:, parity, cols],
                                        z_b[:].rearrange("p g d -> p (g d)")[:, cols], ALU.mult
                                        ).then_inc(sz_ready, 1)

            def sum_wo(c):
                for q in (0, 2):
                    k = 4 * c + q
                    n = k + 4
                    v = stage(n % SLOTS).rearrange("p (g u v d) -> p g u v d", g=2, u=2, v=2)
                    if c >= 2 and q == 0:
                        pool.wait_ge(setup_filled, filled_by(("wo", c - 2, 1)))
                    pool.wait_ge(stage_in[n % SLOTS], 16 * (n // SLOTS + 1))
                    nc.gpsimd.tensor_tensor(v[:, :, :, 0, :], v[:, :, :, 0, :], v[:, :, :, 1, :], ALU.add
                                            ).then_inc(pool_pairs, 1)
                    pool.wait_ge(pool_pairs, k // 2 + 1)
                    nc.gpsimd.tensor_tensor(Wo_sum[:, c % 2, 2 * q:2 * q + 2, :], v[:, :, 0, 0, :],
                                            v[:, :, 1, 0, :], ALU.add).then_inc(pool_summed, 1)

            nc.gpsimd.memset(neg_half[:], -0.5).then_inc(consts_set, 1)
            nc.gpsimd.memset(ident[:], 0.0).then_inc(consts_set, 1)
            pool.wait_ge(consts_set, 2)
            nc.gpsimd.affine_select(out=ident[:], in_=ident[:], compare_op=ALU.not_equal, fill=1.0,
                                    base=0, pattern=[[-1, P]], channel_multiplier=1).then_inc(consts_set, 1)
            rstd_of(0, 0)
            rstd_of(1, 1)
            pool.wait_ge(wscale_in, 16)
            for j in range(2):
                ks = slice(j * K // 2, (j + 1) * K // 2)
                pool.wait_ge(w_cast, j + 1)
                nc.gpsimd.tensor_tensor(wscale[:, ks, :], w_f32[:, ks, :], wscale[:, ks, :], ALU.mult
                                        ).then_inc(wd_ready, 1)

            def s_times_z(t, parity):
                for h in range(2):
                    times_z(t, parity, h)

            s_times_z(0, 0)
            rstd_of(2, 0)
            sum_wo(0)
            rstd_of(3, 1)
            s_times_z(1, 1)
            sum_wo(1)
            rstd_of(4, 0)
            s_times_z(2, 0)
            sum_wo(2)
            rstd_of(5, 1)
            sum_wo(3)
            s_times_z(3, 1)
            for t in range(AHEAD - 1):
                add_b(t)
            with pool.Fori(0, PAIRS) as i:
                for j in range(2):
                    t = AHEAD + 2 * i + j
                    rstd_of(t + 2, j)
                    s_times_z(t, j)
                    add_b(t - 1)
            for t in range(T - 2, T):
                s_times_z(t, t % 2)
                add_b(t - 1)
            add_b(T - 1)

        @block.scalar
        def _(act):
            def copy_xT_hi(t, parity):
                act.wait_ge(xT_filled, t + 1)
                if from_tile(t, 2):
                    act.wait_ge(dense_filled, t - 1)
                nc.scalar.activation(xT_hi[:, parity, :, :].rearrange("p k r -> p (k r)"), xT_ps[:], ACT.Copy
                                     ).then_inc(xT_hi_ready, 1)

            def exp_of(t, parity, h):
                cols = slice(h * HALF, (h + 1) * HALF)
                act.wait_ge(q_biased, 2 * t + h + 1)
                if from_tile(t, 2):
                    act.wait_ge(den_ready, t - 1)
                nc.scalar.activation(ebuf[:, parity, cols], tbuf[:, parity, cols], ACT.Relu, scale=-1.0
                                     ).then_inc(qneg_ready, 1)
                act.wait_ge(qneg_ready, 2 * t + h + 1)
                nc.scalar.activation(ebuf[:, parity, cols], ebuf[:, parity, cols], ACT.Exp, scale=-1.0
                                     ).then_inc(exp_ready, 1)

            def copy_aT_hi(t, parity, h):
                act.wait_ge(aT_filled, 2 * t + h + 1)
                if from_tile(t, 2):
                    act.wait_ge(attn_filled, t - 1)
                nc.scalar.activation(aT_hi[:, parity, h * GH:(h + 1) * GH, :].rearrange("p g r -> p (g r)"),
                                     aT_ps[h][:], ACT.Copy).then_inc(aT_hi_ready, 1)

            def copy_setup(what, out):
                act.wait_ge(setup_filled, filled_by(what))
                nc.scalar.activation(out, setup_bank(what)[:].rearrange("p (g c) -> p g c", g=4), ACT.Copy
                                     ).then_inc(setup_copied, 1)

            def make_a(t, parity):
                if isinstance(t, int) and t == 1:
                    act.wait_ge(setup_filled, filled_by(("m", 0, 1)))
                if isinstance(t, int) and t in (2, 3):
                    act.wait_ge(wd_lo_ready, 2)
                if from_tile(t, 4):
                    act.wait_ge(aT_filled, 2 * t - 2)
                act.wait_ge(rden_ready, t + 1)
                for g in range(G):
                    last = nc.scalar.activation(a[:, a_slot(t, parity), g * D:(g + 1) * D],
                                                tbuf[:, parity, g * D:(g + 1) * D], ACT.Copy,
                                                scale=rden[:, parity, g:g + 1])
                last.then_inc(a_ready, 1)

            def exps_of(t, parity):
                for h in range(2):
                    exp_of(t, parity, h)

            def copy_wd_hi():
                for j in range(2):
                    ks = slice(j * K // 2, (j + 1) * K // 2)
                    act.wait_ge(wd_ready, j + 1)
                    nc.scalar.activation(wd_hi[:, ks, :], wscale[:, ks, :], ACT.Copy).then_inc(wd_hi_ready, 1)

            def copy_wo(c):
                for h in range(2):
                    if c >= 2:
                        act.wait_ge(setup_filled, filled_by(("p", c - 2, 1)))
                    copy_setup(("wo", c, h), WoT[:, c % 2, h * GH:(h + 1) * GH, :])

            def copy_P_hi(c):
                for h in range(2):
                    copy_setup(("p", c, h), P_hi[:, h * GH:(h + 1) * GH, c * P:(c + 1) * P])

            def copy_a(t, parity):
                for h in range(2):
                    copy_aT_hi(t, parity, h)

            copy_xT_hi(0, 0)
            for h in range(2):
                for k in range(K):
                    copy_setup(("wq", h, k),
                               WqT_hi[:, k, h * HALF:(h + 1) * HALF].rearrange("p (g c) -> p g c", g=4))
            act.wait_ge(w_in, 16)
            for j in range(2):
                ks = slice(j * K // 2, (j + 1) * K // 2)
                nc.scalar.activation(w_f32[:, ks, :], w_i8[:, ks, :], ACT.Copy).then_inc(w_cast, 1)
            copy_xT_hi(1, 1)
            exps_of(0, 0)
            copy_wd_hi()
            exps_of(1, 1)
            for h in range(2):
                copy_setup(("m", 0, h), MT[:, h * GH:(h + 1) * GH, :])
            copy_xT_hi(2, 0)
            make_a(0, 0)
            copy_xT_hi(3, 1)
            copy_wo(0)
            exp_of(2, 0, 0)
            make_a(1, 1)
            exp_of(2, 0, 1)
            copy_P_hi(0)
            copy_wo(1)
            copy_xT_hi(4, 0)
            exp_of(3, 1, 0)
            copy_P_hi(1)
            copy_wo(2)
            make_a(2, 0)
            exp_of(3, 1, 1)
            copy_P_hi(2)
            copy_wo(3)
            copy_P_hi(3)
            copy_a(0, 0)
            copy_a(1, 1)
            copy_a(2, 0)
            with act.Fori(0, PAIRS) as i:
                for j in range(2):
                    t = AHEAD + 2 * i + j
                    copy_xT_hi(t + 1, 1 - j)
                    exp_of(t, j, 0)
                    make_a(t - 1, 1 - j)
                    exp_of(t, j, 1)
                    copy_a(t - 1, 1 - j)
            for t in range(T - 2, T):
                if t + 1 < T:
                    copy_xT_hi(t + 1, (t + 1) % 2)
                exp_of(t, t % 2, 0)
                make_a(t - 1, (t - 1) % 2)
                exp_of(t, t % 2, 1)
                copy_a(t - 1, (t - 1) % 2)
            make_a(T - 1, (T - 1) % 2)
            copy_a(T - 1, (T - 1) % 2)

        @block.vector
        def _(dve):
            def statistics(t, parity):
                wait_x(dve, t, parity)
                nc.vector.bn_stats(stats[:], tile(t)).then_inc(stats_set, 1)

            def mean_and_variance(t, parity):
                nc.vector.bn_aggr(meanvar[:, parity, :], stats[:]).then_inc(meanvar_ready, 1)

            def variance_eps(t, parity):
                dve.wait_ge(meanvar_ready, t + 1)
                if from_tile(t, 2):
                    dve.wait_ge(rstd_ready, t - 1)
                nc.vector.tensor_scalar_add(vareps[:, parity, :], meanvar[:, parity, 1:2], LN_EPS
                                            ).then_inc(vareps_ready, 1)

            def normalise(t, parity):
                dve.wait_ge(rstd_ready, t + 1)
                if from_tile(t, 1):
                    dve.wait_ge(xT_filled, t)
                nc.vector.tensor_scalar(xn[:], tile(t), meanvar[:, parity, 0:1], rstd[:, parity, :],
                                        ALU.subtract, ALU.mult).then_inc(xn_ready, 1)

            def split_xT_lo(t, parity):
                dve.wait_ge(xT_hi_ready, t + 1)
                if from_tile(t, 2):
                    dve.wait_ge(dense_filled, t - 1)
                nc.vector.tensor_tensor(xT_lo[:, parity, :, :].rearrange("p k r -> p (k r)"), xT_ps[:],
                                        xT_hi[:, parity, :, :].rearrange("p k r -> p (k r)").bitcast(F32),
                                        ALU.subtract).then_inc(xT_lo_ready, 1)

            def setup_lo(what, out, hi):
                dve.wait_ge(setup_copied, filled_by(what))
                nc.vector.tensor_tensor(out, setup_bank(what)[:].rearrange("p (g c) -> p g c", g=4),
                                        hi.bitcast(F32), ALU.subtract).then_inc(setup_lo_ready, 1)

            def add_bias(t, parity, h):
                cols = slice(h * HALF, (h + 1) * HALF)
                if isinstance(t, int) and t == 0 and h == 0:
                    dve.wait_ge(bq_in, 16)
                if h == 0 and from_tile(t, 2):
                    dve.wait_ge(a_ready, t - 1)
                dve.wait_ge(q_filled, 2 * t + h + 1)
                nc.vector.tensor_tensor(tbuf[:, parity, cols], q_ps[h][:],
                                        bq_b[:].rearrange("p g d -> p (g d)")[:, cols], ALU.add
                                        ).then_inc(q_biased, 1)

            def make_s(t, parity, h):
                cols = slice(h * HALF, (h + 1) * HALF)
                dve.wait_ge(exp_ready, 2 * t + h + 1)
                nc.vector.scalar_tensor_tensor(tbuf[:, parity, cols], tbuf[:, parity, cols], 0.0,
                                               ebuf[:, parity, cols], ALU.max, ALU.add).then_inc(s_ready, 1)

            def denominator(t, parity):
                dve.wait_ge(sz_ready, 2 * t + 2)
                nc.vector.reduce_sum(den[:], ebuf[:, parity, :].rearrange("p (g d) -> p g d", g=G), AX.X
                                     ).then_inc(den_ready, 1)
                dve.wait_ge(den_ready, t + 1)
                nc.vector.tensor_scalar_add(den_e[:], den[:], DEN_EPS).then_inc(den_e_ready, 1)
                dve.wait_ge(den_e_ready, t + 1)
                nc.vector.reciprocal(rden[:, parity, :], den_e[:]).then_inc(rden_ready, 1)

            def add_dense(t):
                dve.wait_ge(dense_filled, t + 1)
                nc.vector.tensor_tensor(tile(t), dense_ps[:], tile(t), ALU.add).then_inc(dense_added, 1)

            def split_aT_lo(t, parity, h):
                gs = slice(h * GH, (h + 1) * GH)
                dve.wait_ge(aT_hi_ready, 2 * t + h + 1)
                if from_tile(t, 2):
                    dve.wait_ge(attn_filled, t - 1)
                nc.vector.tensor_tensor(aT_lo[:, parity, gs, :].rearrange("p g r -> p (g r)"), aT_ps[h][:],
                                        aT_hi[:, parity, gs, :].rearrange("p g r -> p (g r)").bitcast(F32),
                                        ALU.subtract).then_inc(aT_lo_ready, 1)

            def add_attn(t):
                dve.wait_ge(attn_filled, t + 1)
                dve.wait_ge(b_added, t + 1)
                nc.vector.tensor_tensor(tile(t), attn_ps[:], tile(t), ALU.add).then_inc(attn_added, 1)

            def sum_wo(c):
                for q in (1, 3):
                    k = 4 * c + q
                    n = k + 4
                    v = stage(n % SLOTS).rearrange("p (g u v d) -> p g u v d", g=2, u=2, v=2)
                    if c >= 2 and q == 1:
                        dve.wait_ge(setup_filled, filled_by(("wo", c - 2, 1)))
                    dve.wait_ge(stage_in[n % SLOTS], 16 * (n // SLOTS + 1))
                    nc.vector.tensor_tensor(v[:, :, :, 0, :], v[:, :, :, 0, :], v[:, :, :, 1, :], ALU.add
                                            ).then_inc(dve_pairs, 1)
                    dve.wait_ge(dve_pairs, k // 2 + 1)
                    nc.vector.tensor_tensor(Wo_sum[:, c % 2, 2 * q:2 * q + 2, :], v[:, :, 0, 0, :],
                                            v[:, :, 1, 0, :], ALU.add).then_inc(dve_summed, 1)

            def P_split(c):
                for h in range(2):
                    gs, ns = slice(h * GH, (h + 1) * GH), slice(c * P, (c + 1) * P)
                    setup_lo(("p", c, h), P_lo[:, gs, ns], P_hi[:, gs, ns])

            def statistics_at_once(t):
                statistics(t, t % 2)
                dve.wait_ge(stats_set, t + 1)
                mean_and_variance(t, t % 2)
                variance_eps(t, t % 2)

            def split_wq_lo(h, k):
                cs = slice(h * HALF, (h + 1) * HALF)
                setup_lo(("wq", h, k), WqT_lo[:, k, cs].rearrange("p (g c) -> p g c", g=4),
                         WqT_hi[:, k, cs].rearrange("p (g c) -> p g c", g=4))

            def split_wd_lo():
                for j in range(2):
                    ks = slice(j * K // 2, (j + 1) * K // 2)
                    dve.wait_ge(wd_hi_ready, j + 1)
                    nc.vector.tensor_tensor(wd_lo[:, ks, :], wscale[:, ks, :], wd_hi[:, ks, :].bitcast(F32),
                                            ALU.subtract).then_inc(wd_lo_ready, 1)

            def make_s_both(t, parity):
                for h in range(2):
                    make_s(t, parity, h)

            def split_a(t, parity):
                for h in range(2):
                    split_aT_lo(t, parity, h)

            def q_step(t, parity, stats_ahead=True, next_x=True):
                if stats_ahead:
                    statistics(t + 2, parity)
                    dve.wait_ge(stats_set, t + 3)
                add_bias(t, parity, 0)
                if stats_ahead:
                    mean_and_variance(t + 2, parity)
                    variance_eps(t + 2, parity)
                denominator(t - 1, 1 - parity)
                if next_x:
                    split_xT_lo(t + 1, 1 - parity)
                if isinstance(t, int) and t == AHEAD - 1:
                    P_split(1)
                add_bias(t, parity, 1)
                if stats_ahead:
                    normalise(t + 2, parity)
                if isinstance(t, int) and t < AHEAD:
                    sum_wo(t - 1 if t == 2 else 3)
                make_s_both(t, parity)
                if isinstance(t, int) and t == AHEAD - 1:
                    P_split(2)
                add_dense(t)

            statistics_at_once(0)
            normalise(0, 0)
            split_xT_lo(0, 0)
            for k in range(K):
                split_wq_lo(0, k)
            statistics_at_once(1)
            split_wq_lo(1, 0)
            normalise(1, 1)
            for k in range(1, K):
                split_wq_lo(1, k)
            add_bias(0, 0, 0)
            split_xT_lo(1, 1)
            add_bias(0, 0, 1)
            statistics_at_once(2)
            make_s_both(0, 0)
            add_bias(1, 1, 0)
            split_wd_lo()
            add_bias(1, 1, 1)
            normalise(2, 0)
            denominator(0, 0)
            add_dense(0)
            sum_wo(0)
            split_xT_lo(2, 0)
            statistics_at_once(3)
            normalise(3, 1)
            make_s_both(1, 1)
            add_dense(1)
            q_step(2, 0)
            P_split(0)
            sum_wo(2)
            q_step(3, 1)
            P_split(3)
            split_a(0, 0)
            split_a(1, 1)
            add_attn(0)
            split_a(2, 0)
            add_attn(1)
            with dve.Fori(0, PAIRS) as i:
                for j in range(2):
                    t = AHEAD + 2 * i + j
                    q_step(t, j)
                    split_a(t - 1, 1 - j)
                    add_attn(t - 2)
            for t in range(T - 2, T):
                q_step(t, t % 2, stats_ahead=False, next_x=t + 1 < T)
                split_a(t - 1, (t - 1) % 2)
                if t == T - 1:
                    denominator(t, t % 2)
                add_attn(t - 2)
            split_a(T - 1, (T - 1) % 2)
            add_attn(T - 2)
            add_attn(T - 1)

        @block.tensor
        def _(pe):
            def transpose_x(t):
                if isinstance(t, int) and t == 0:
                    pe.wait_ge(consts_set, 3)
                pe.wait_ge(xn_ready, t + 1)
                if from_tile(t, 1):
                    pe.wait_ge(xT_lo_ready, t)
                for k in range(K):
                    last = nc.tensor.transpose(xT_ps[:, k * P:(k + 1) * P], xn[:, k * P:(k + 1) * P], ident[:])
                last.then_inc(xT_filled, 1)

            def three_passes(out, x_hi, x_lo, w_hi, w_lo, start, stop):
                nc.tensor.matmul(out, x_hi, w_hi, start=start, stop=False)
                nc.tensor.matmul(out, x_hi, w_lo, start=False, stop=False)
                return nc.tensor.matmul(out, x_lo, w_hi, start=False, stop=stop)

            def q_chunk(parity, h, k):
                cols = slice(h * HALF, (h + 1) * HALF)
                return three_passes(q_ps[h][:], xT_hi[:, parity, k, :], xT_lo[:, parity, k, :],
                                    WqT_hi[:, k, cols], WqT_lo[:, k, cols], k == 0, k == K - 1)

            def product_q(t, parity, h):
                pe.wait_ge(xT_lo_ready, t + 1)
                if from_tile(t, 1):
                    pe.wait_ge(q_biased, 2 * t - 1 + h)
                for k in range(K):
                    last = q_chunk(parity, h, k)
                last.then_inc(q_filled, 1)

            def product_dense(t, parity):
                if from_tile(t, 1):
                    pe.wait_ge(dense_added, t)
                for k in range(K):
                    if isinstance(t, int) and t == 0:
                        pe.wait_ge(wd_lo_ready, 2 * k // K + 1)
                    last = three_passes(dense_ps[:], xT_hi[:, parity, k, :], xT_lo[:, parity, k, :],
                                        wd_hi[:, k, :], wd_lo[:, k, :], k == 0, k == K - 1)
                last.then_inc(dense_filled, 1)

            def transpose_a(t, parity):
                pe.wait_ge(a_ready, t + 1)
                if isinstance(t, int) and t == 0:
                    pe.wait_ge(setup_copied, filled_by(("wo", NC - 1, 1)))
                for h in range(2):
                    if from_tile(t, 1):
                        pe.wait_ge(aT_lo_ready, 2 * t - 1 + h)
                    for i in range(GH):
                        g = h * GH + i
                        last = nc.tensor.transpose(aT_ps[h][:, i * P:(i + 1) * P],
                                                   a[:, a_slot(t, parity), g * D:(g + 1) * D], ident[:])
                    last.then_inc(aT_filled, 1)

            def product_attn(t, parity):
                if from_tile(t, 1):
                    pe.wait_ge(attn_added, t)
                for g in range(G):
                    if g % GH == 0:
                        h = g // GH
                        pe.wait_ge(aT_lo_ready, 2 * t + h + 1)
                        if isinstance(t, int) and t == 0:
                            pe.wait_ge(setup_lo_ready, lo_by(("p", NC - 1, h)))
                    last = three_passes(attn_ps[:], aT_hi[:, parity, g, :], aT_lo[:, parity, g, :],
                                        P_hi[:, g, :], P_lo[:, g, :], g == 0, g == G - 1)
                last.then_inc(attn_filled, 1)

            def setup_free(what):
                before = [v for v in SETUP[:USE[what]] if setup_bank(v) is setup_bank(what)]
                if what[:2] == ("p", NC - 1):
                    pe.wait_ge(q_biased, 2 * AHEAD)
                elif before and before[-1][0] in ("wq", "p"):
                    pe.wait_ge(setup_lo_ready, lo_by(before[-1]))
                elif before:
                    pe.wait_ge(setup_copied, filled_by(before[-1]))

            def transposes(what, blocks):
                setup_free(what)
                for i, block_in in enumerate(blocks):
                    last = nc.tensor.transpose(setup_bank(what)[:, i * P:(i + 1) * P], block_in, ident[:])
                last.then_inc(setup_filled, 1)

            def transpose_wq(h, k):
                if k == 0:
                    for i in (2 * h, 2 * h + 1):
                        pe.wait_ge(stage_in[i], 16)
                transposes(("wq", h, k), [stage(2 * h + i // 2)[:, (i % 2) * HID + k * P:(i % 2) * HID + (k + 1) * P]
                                          for i in range(GH)])

            def transpose_m():
                pe.wait_ge(M_in, 16)
                for h in range(2):
                    transposes(("m", 0, h), [M_sb[:, h * GH + i, :] for i in range(GH)])

            def transpose_wo(c):
                pe.wait_ge(pool_summed, 2 * c + 2)
                pe.wait_ge(dve_summed, 2 * c + 2)
                for h in range(2):
                    transposes(("wo", c, h), [Wo_sum[:, c % 2, h * GH + i, :] for i in range(GH)])

            def product_P(c):
                for h in range(2):
                    pe.wait_ge(setup_copied, filled_by(("wo", c, h)))
                    setup_free(("p", c, h))
                    for i in range(GH):
                        g = h * GH + i
                        last = nc.tensor.matmul(setup_bank(("p", c, h))[:, i * P:(i + 1) * P], MT[:, g, :],
                                                WoT[:, c % 2, g, :], start=True, stop=True)
                    last.then_inc(setup_filled, 1)

            transpose_x(0)
            for k in range(K):
                transpose_wq(0, k)
            for k in range(2):
                transpose_wq(1, k)
            pe.wait_ge(xT_lo_ready, 1)
            for h in range(2):
                for k in range(K):
                    pe.wait_ge(setup_lo_ready, lo_by(("wq", h, k)))
                    if h == 0 and k < 2:
                        transpose_wq(1, 2 + k)
                    if h == 1 and k == 0:
                        pe.wait_ge(setup_lo_ready, lo_by(("wq", 1, 1)))
                    last = q_chunk(0, h, k)
                    if k == K - 1:
                        last.then_inc(q_filled, 1)
                    if h == 1 and k == 1:
                        transpose_x(1)
            for h in range(2):
                product_q(1, 1, h)
            transpose_m()
            product_dense(0, 0)
            transpose_x(2)
            product_dense(1, 1)
            product_q(2, 0, 0)
            transpose_x(3)
            transpose_wo(0)
            product_q(2, 0, 1)
            product_P(0)
            product_dense(2, 0)
            transpose_wo(1)
            product_q(3, 1, 0)
            transpose_x(4)
            product_P(1)
            transpose_wo(2)
            product_q(3, 1, 1)
            product_P(2)
            transpose_wo(3)
            product_dense(3, 1)
            product_P(3)
            transpose_a(0, 0)
            transpose_a(1, 1)
            product_attn(0, 0)
            transpose_a(2, 0)
            product_attn(1, 1)
            with pe.Fori(0, PAIRS) as i:
                for j in range(2):
                    t = AHEAD + 2 * i + j
                    product_q(t, j, 0)
                    transpose_x(t + 1)
                    product_q(t, j, 1)
                    product_dense(t, j)
                    transpose_a(t - 1, 1 - j)
                    product_attn(t - 2, j)
            for t in range(T - 2, T):
                product_q(t, t % 2, 0)
                if t + 1 < T:
                    transpose_x(t + 1)
                product_q(t, t % 2, 1)
                product_dense(t, t % 2)
                transpose_a(t - 1, (t - 1) % 2)
                product_attn(t - 2, t % 2)
            transpose_a(T - 1, (T - 1) % 2)
            for t in range(T - 2, T):
                product_attn(t, t % 2)


_INS = ["L0_attn_hidden_states", "L0_attn_Wq", "L0_attn_bq", "L0_attn_Wo", "L0_attn_M", "L0_attn_z",
        "L0_ffn_w", "L0_ffn_w_scale", "L0_ffn_b"]


def kernel(**inputs):
    import numpy as np
    import concourse.bacc as bacc
    from concourse.bass_utils import run_bass_kernel_spmd

    nc = bacc.Bacc("TRN2", target_bir_lowering=False, num_devices=1)
    arrays, args = {}, []
    for name in _INS:
        v = np.ascontiguousarray(inputs[name])
        if v.dtype == np.int8:
            v = v.view(np.int32)
        arrays[f"in_{name}"] = v
        args.append(nc.dram_tensor(f"in_{name}", v.shape, mybir.dt.from_np(v.dtype), kind="ExternalInput").ap())
    shape = inputs["L0_attn_hidden_states"].shape
    out = nc.dram_tensor("out", shape, F32, kind="ExternalOutput").ap()
    retrieval_and_dense(nc, *args, out)
    result = run_bass_kernel_spmd(nc, [arrays], core_ids=[0])
    return result.results[0]["out"]
```

```python
from contextlib import ExitStack

import concourse.bass as bass
from concourse import mybir

F32 = mybir.dt.float32
F32R = mybir.dt.float32r
I8 = mybir.dt.int8
I32 = mybir.dt.int32
ALU = mybir.AluOpType
ACT = mybir.ActivationFunctionType
AX = mybir.AxisListType

LN_EPS = 1e-5
DEN_EPS = 1e-6


def retrieval_and_dense(nc, x_d, Wq_d, bq_d, Wo_d, M_d, z_d, w_d, wscale_d, b_d, out_d):
    P = 128
    HID = x_d.shape[-1]
    G, D, _ = M_d.shape
    R = Wq_d.shape[0] // (G * D)
    K = HID // P
    E = G * D
    HALF = E // 2
    GH = G // 2
    NC = HID // P
    xr = x_d.rearrange("b s c -> (b s) c")
    T = xr.shape[0] // P
    WARM_UP = 9
    AHEAD = 4
    LAG = 2
    SLOTS = 6
    LENT = SLOTS - 1
    PAIRS = (T - 2 - AHEAD) // 2
    EARLY = T - 2 * LENT
    assert P == D and HID == 512 and HALF == 512 and R == 4 and T == 16 and AHEAD < EARLY

    x_t = xr.rearrange("(t p) c -> t p c", p=P)
    out_t = out_d.rearrange("b s c -> (b s) c").rearrange("(t p) c -> t p c", p=P)
    wq_t = Wq_d.rearrange("(g r p) c -> p g r c", r=R, p=P)
    bq_g = bq_d.rearrange("(g r d) -> g r d", r=R, d=D)[:, 0, :]

    with ExitStack() as ctx:
        def sb(name, shape, dt=F32):
            return ctx.enter_context(nc.sbuf_tensor(name, shape, dt))

        def bank(name):
            return ctx.enter_context(nc.psum_tensor(name, [P, 512], F32))

        def sem(name):
            return ctx.enter_context(nc.semaphore(name))

        x = sb("x", [P, T, HID])
        xn = sb("xn", [P, HID])
        xT_hi = sb("xT_hi", [P, 2, K, P], F32R)
        xT_lo = sb("xT_lo", [P, 2, K, P], F32R)
        WqT_hi = sb("WqT_hi", [P, K, E], F32R)
        WqT_lo = sb("WqT_lo", [P, K, E], F32R)
        wd_hi = sb("wd_hi", [P, K, HID], F32R)
        wd_lo = sb("wd_lo", [P, K, HID], F32R)
        P_hi = sb("P_hi", [P, G, HID], F32R)
        P_lo = sb("P_lo", [P, G, HID], F32R)
        bq_b = sb("bq_b", [P, G, D])
        z_b = sb("z_b", [P, G, D])
        b_b = sb("b_b", [P, HID])
        tbuf = sb("tbuf", [P, 2, E])
        ebuf = sb("ebuf", [P, 2, E])
        a = sb("a", [P, 4, E])
        aT_hi = sb("aT_hi", [P, 2, G, P], F32R)
        aT_lo = sb("aT_lo", [P, 2, G, P], F32R)
        Wo_sum = sb("Wo_sum", [P, 2, G, D])
        WoT = sb("WoT", [P, 2, G, P])
        MT = sb("MT", [P, G, D])
        stage_own = sb("stage_own", [P, 2 * HID])
        w_words = sb("w_words", [P, K, HID // 4], I32)
        w_i8 = w_words[:].bitcast(I8)
        ident = sb("ident", [P, P])
        neg_half = sb("neg_half", [P, 1])
        stats = sb("stats", [P, 6])
        meanvar = sb("meanvar", [P, 2, 2])
        vareps = sb("vareps", [P, 2, 1])
        rstd = sb("rstd", [P, 2, 1])
        den = sb("den", [P, G])
        den_e = sb("den_e", [P, G])
        rden = sb("rden", [P, 2, G])

        def stage(slot):
            if slot >= LENT:
                return stage_own[:]
            return x[:, EARLY + 2 * slot:EARLY + 2 * slot + 2, :].rearrange("p t c -> p (t c)")

        wscale = a[:, 0:2, :].rearrange("p s (k n) -> p (s k) n", n=HID)
        w_f32 = Wo_sum[:].rearrange("p c g d -> p (c g d)").rearrange("p (k n) -> p k n", n=HID)
        warm = tbuf[:, 1, 0:P]
        M_sb = a[:, 3, :].rearrange("p (g e) -> p g e", g=G)

        def a_slot(t, parity):
            return 2 + parity if isinstance(t, int) and t < LAG else parity

        xT_ps = bank("xT_ps")
        q_ps = [bank("q0_ps"), bank("q1_ps")]
        dense_ps = bank("dense_ps")
        aT_ps = [bank("aT0_ps"), bank("aT1_ps")]
        attn_ps = [bank("attn0_ps"), bank("attn1_ps")]

        def last_attn_ps(c):
            return [attn_ps[(T - 1) % 2], q_ps[0]][c][:, 0:HID // 2]

        x_in = [sem(f"x_in{t}") for t in range(EARLY)]
        x_rest_in = sem("x_rest_in")
        stage_in = [sem(f"stage_in{s}") for s in range(SLOTS)]
        w_in, wscale_in, bq_in, z_in, b_in, M_in = (
            sem(n) for n in ("w_in", "wscale_in", "bq_in", "z_in", "b_in", "M_in"))
        warm_set = sem("warm_set")
        consts_set = sem("consts_set")
        stats_set = sem("stats_set")
        meanvar_ready = sem("meanvar_ready")
        vareps_ready = sem("vareps_ready")
        rstd_ready = sem("rstd_ready")
        xn_ready = sem("xn_ready")
        xT_filled = sem("xT_filled")
        xT_hi_ready = sem("xT_hi_ready")
        xT_lo_ready = sem("xT_lo_ready")
        setup_filled = sem("setup_filled")
        setup_copied = sem("setup_copied")
        setup_lo_ready = sem("setup_lo_ready")
        w_cast = sem("w_cast")
        wd_first_ready = sem("wd_first_ready")
        wd_second_ready = sem("wd_second_ready")
        wd_hi_ready = sem("wd_hi_ready")
        wd_lo_ready = sem("wd_lo_ready")
        pool_pairs = sem("pool_pairs")
        pool_summed = sem("pool_summed")
        dve_pairs = sem("dve_pairs")
        dve_summed = sem("dve_summed")
        q_filled = sem("q_filled")
        q_biased = sem("q_biased")
        qneg_ready = sem("qneg_ready")
        exp_ready = sem("exp_ready")
        s_ready = sem("s_ready")
        sz_ready = sem("sz_ready")
        den_ready = sem("den_ready")
        den_e_ready = sem("den_e_ready")
        rden_ready = sem("rden_ready")
        a_ready = sem("a_ready")
        b_added = sem("b_added")
        dense_filled = sem("dense_filled")
        dense_added = sem("dense_added")
        aT_filled = sem("aT_filled")
        aT_hi_ready = sem("aT_hi_ready")
        aT_lo_ready = sem("aT_lo_ready")
        attn_filled = sem("attn_filled")
        attn_added = sem("attn_added")
        stored = sem("stored")

        block = ctx.enter_context(nc.Block())

        SETUP = [("wq", h, k) for h in range(2) for k in range(K)] + [("m", 0, h) for h in range(2)]
        SETUP += [(kind, c, h) for c in range(NC) for kind in ("wo", "p") for h in range(2)]
        USE = {what: u for u, what in enumerate(SETUP)}

        def setup_bank(what):
            kind, c, h = what
            if kind == "wq":
                return [aT_ps[0], aT_ps[1], attn_ps[0], attn_ps[1], dense_ps, q_ps[1], aT_ps[0], aT_ps[1]][USE[what]]
            if kind == "wo":
                return aT_ps[h]
            if what[:2] == ("p", NC - 1):
                return q_ps[1 - h]
            return attn_ps[h]

        def filled_by(what):
            return USE[what] + 1

        def lo_by(what):
            return sum(1 for v in SETUP[:USE[what] + 1] if v[0] in ("wq", "p"))

        def from_tile(t, n):
            return t >= n if isinstance(t, int) else True

        def tile(t):
            return x[:, bass.ds(t, 1), :].rearrange("p a c -> p (a c)")

        def wait_x(eng, t, parity):
            if isinstance(t, int) and t < EARLY:
                eng.wait_ge(x_in[t], 16)
            else:
                eng.wait_ge(x_rest_in, 8 * (t - parity) - 8 * EARLY + 16)

        @block.sync
        def _(sp):
            def load_x(t):
                sp.dma_start(x[:, t, :], x_t[t]).then_inc(x_in[t], 16)

            def load_wq(i):
                h, ks = i // 2, slice((i % 2) * HID // 2, (i % 2 + 1) * HID // 2)
                sp.dma_start(stage(i).rearrange("p (g c) -> p g c", g=GH),
                             wq_t[:, h * GH:(h + 1) * GH, 0, ks]).then_inc(stage_in[i], 16)

            def load_wo(k):
                n = k + 4
                c, q = k // 4, k % 4
                if n - SLOTS >= 4:
                    old = n - SLOTS - 4
                    sp.wait_ge(pool_summed if old % 2 == 0 else dve_summed, old // 2 + 1)
                elif n >= SLOTS:
                    i = n - SLOTS
                    sp.wait_ge(setup_filled, filled_by(("wq", i // 2, (i % 2 + 1) * K // 2 - 1)))
                sp.dma_start(stage(n % SLOTS),
                             Wo_d[c * P:(c + 1) * P, q * 2 * R * D:(q + 1) * 2 * R * D]
                             ).then_inc(stage_in[n % SLOTS], 16)

            load_x(0)
            load_wq(0)
            load_wq(1)
            load_wq(2)
            load_wq(3)
            load_x(1)
            sp.dma_start(w_words[:], w_d.rearrange("(k p) n -> p k n", p=P)).then_inc(w_in, 16)
            sp.dma_start(bq_b[:], bq_g.unsqueeze(0).to_broadcast([P, G, D])).then_inc(bq_in, 16)
            sp.dma_start(wscale, wscale_d.rearrange("(k p) n -> p k n", p=P)).then_inc(wscale_in, 16)
            load_x(2)
            sp.dma_start(z_b[:], z_d.unsqueeze(0).to_broadcast([P, G, D])).then_inc(z_in, 16)
            sp.dma_start(b_b[:], b_d.unsqueeze(0).to_broadcast([P, HID])).then_inc(b_in, 16)
            sp.dma_start(M_sb, M_d.rearrange("g d e -> d g e")).then_inc(M_in, 16)
            load_x(3)
            for k in range(4 * NC):
                load_wo(k)
                if k == 4:
                    load_x(4)
                if k == 9:
                    load_x(5)
            for s in range(LENT):
                last = max(k for k in range(4 * NC) if (k + 4) % SLOTS == s)
                sp.wait_ge(pool_summed if last % 2 == 0 else dve_summed, last // 2 + 1)
                t = EARLY + 2 * s
                sp.dma_start(x[:, t:t + 2, :], x_t[t:t + 2].rearrange("t p c -> p t c")
                             ).then_inc(x_rest_in, 16)
                sp.wait_ge(x_rest_in, 16 * (s + 1))
            with sp.Fori(0, T - 1) as t:
                sp.wait_ge(attn_added, t + 1)
                sp.dma_start(out_t[bass.ds(t, 1)].rearrange("t p c -> p (t c)"), tile(t)).then_inc(stored, 16)
            for c in range(2):
                cols = slice(c * HID // 2, (c + 1) * HID // 2)
                sp.wait_ge(attn_added, T + c)
                sp.dma_start(out_t[T - 1][:, cols], x[:, T - 1, cols]).then_inc(stored, 16)
            sp.wait_ge(stored, 16 * (T + 1))

        @block.gpsimd
        def _(pool):
            def rstd_of(t, parity):
                pool.wait_ge(vareps_ready, t + 1)
                if from_tile(t, 2):
                    pool.wait_ge(xn_ready, t - 1)
                nc.gpsimd.tensor_tensor(rstd[:, parity, :], vareps[:, parity, :], neg_half[:], ALU.pow
                                        ).then_inc(rstd_ready, 1)

            def add_b(t):
                if isinstance(t, int) and t == 0:
                    pool.wait_ge(b_in, 16)
                pool.wait_ge(dense_added, t + 1)
                nc.gpsimd.tensor_tensor(tile(t), tile(t), b_b[:], ALU.add).then_inc(b_added, 1)

            def times_z(t, parity, h):
                cols = slice(h * HALF, (h + 1) * HALF)
                if isinstance(t, int) and t == 0 and h == 0:
                    pool.wait_ge(z_in, 16)
                pool.wait_ge(s_ready, 2 * t + h + 1)
                nc.gpsimd.tensor_tensor(ebuf[:, parity, cols], tbuf[:, parity, cols],
                                        z_b[:].rearrange("p g d -> p (g d)")[:, cols], ALU.mult
                                        ).then_inc(sz_ready, 1)

            def sum_wo(c, pieces=(0, 2)):
                for q in pieces:
                    k = 4 * c + q
                    n = k + 4
                    v = stage(n % SLOTS).rearrange("p (g u v d) -> p g u v d", g=2, u=2, v=2)
                    if c >= 2 and q == 0:
                        pool.wait_ge(setup_filled, filled_by(("wo", c - 2, 1)))
                    pool.wait_ge(stage_in[n % SLOTS], 16 * (n // SLOTS + 1))
                    nc.gpsimd.tensor_tensor(v[:, :, :, 0, :], v[:, :, :, 0, :], v[:, :, :, 1, :], ALU.add
                                            ).then_inc(pool_pairs, 1)
                    pool.wait_ge(pool_pairs, k // 2 + 1)
                    nc.gpsimd.tensor_tensor(Wo_sum[:, c % 2, 2 * q:2 * q + 2, :], v[:, :, 0, 0, :],
                                            v[:, :, 1, 0, :], ALU.add).then_inc(pool_summed, 1)

            nc.gpsimd.memset(neg_half[:], -0.5).then_inc(consts_set, 1)
            nc.gpsimd.memset(ident[:], 0.0).then_inc(consts_set, 1)
            pool.wait_ge(consts_set, 2)
            nc.gpsimd.affine_select(out=ident[:], in_=ident[:], compare_op=ALU.not_equal, fill=1.0,
                                    base=0, pattern=[[-1, P]], channel_multiplier=1).then_inc(consts_set, 1)
            rstd_of(0, 0)
            rstd_of(1, 1)
            pool.wait_ge(wscale_in, 16)
            pool.wait_ge(w_cast, K // 2)
            nc.gpsimd.tensor_tensor(wscale[:, :K // 2, :], w_f32[:, :K // 2, :], wscale[:, :K // 2, :], ALU.mult
                                    ).then_inc(wd_first_ready, 1)

            def s_times_z(t, parity):
                for h in range(2):
                    times_z(t, parity, h)

            rstd_of(2, 0)
            sum_wo(0)
            rstd_of(3, 1)
            s_times_z(0, 0)
            sum_wo(1, pieces=(0,))
            s_times_z(1, 1)
            sum_wo(1, pieces=(2,))
            rstd_of(4, 0)
            sum_wo(2)
            times_z(2, 0, 0)
            sum_wo(3, pieces=(0,))
            times_z(2, 0, 1)
            sum_wo(3, pieces=(2,))
            rstd_of(5, 1)
            s_times_z(3, 1)
            for t in range(AHEAD - 1):
                add_b(t)
            with pool.Fori(0, PAIRS) as i:
                for j in range(2):
                    t = AHEAD + 2 * i + j
                    rstd_of(t + 2, j)
                    s_times_z(t, j)
                    add_b(t - 1)
            for t in range(T - 2, T):
                s_times_z(t, t % 2)
                add_b(t - 1)
            add_b(T - 1)

        @block.scalar
        def _(act):
            def copy_xT_hi(t, parity):
                act.wait_ge(xT_filled, t + 1)
                if from_tile(t, 2):
                    act.wait_ge(dense_filled, t - 1)
                nc.scalar.activation(xT_hi[:, parity, :, :].rearrange("p k r -> p (k r)"), xT_ps[:], ACT.Copy
                                     ).then_inc(xT_hi_ready, 1)

            def exp_of(t, parity, h):
                cols = slice(h * HALF, (h + 1) * HALF)
                act.wait_ge(q_biased, 2 * t + h + 1)
                if from_tile(t, 2):
                    act.wait_ge(den_ready, t - 1)
                nc.scalar.activation(ebuf[:, parity, cols], tbuf[:, parity, cols], ACT.Relu, scale=-1.0
                                     ).then_inc(qneg_ready, 1)
                act.wait_ge(qneg_ready, 2 * t + h + 1)
                nc.scalar.activation(ebuf[:, parity, cols], ebuf[:, parity, cols], ACT.Exp, scale=-1.0
                                     ).then_inc(exp_ready, 1)

            def copy_aT_hi(t, parity, h):
                act.wait_ge(aT_filled, 2 * t + h + 1)
                if from_tile(t, 2):
                    act.wait_ge(attn_filled, t - 1)
                nc.scalar.activation(aT_hi[:, parity, h * GH:(h + 1) * GH, :].rearrange("p g r -> p (g r)"),
                                     aT_ps[h][:], ACT.Copy).then_inc(aT_hi_ready, 1)

            def copy_setup(what, out):
                act.wait_ge(setup_filled, filled_by(what))
                nc.scalar.activation(out, setup_bank(what)[:].rearrange("p (g c) -> p g c", g=4), ACT.Copy
                                     ).then_inc(setup_copied, 1)

            def make_a(t, parity):
                if isinstance(t, int) and t == 1:
                    act.wait_ge(setup_filled, filled_by(("m", 0, 1)))
                if isinstance(t, int) and t in (2, 3):
                    act.wait_ge(wd_lo_ready, 2)
                if from_tile(t, 4):
                    act.wait_ge(aT_filled, 2 * t - 2)
                act.wait_ge(rden_ready, t + 1)
                for g in range(G):
                    last = nc.scalar.activation(a[:, a_slot(t, parity), g * D:(g + 1) * D],
                                                tbuf[:, parity, g * D:(g + 1) * D], ACT.Copy,
                                                scale=rden[:, parity, g:g + 1])
                last.then_inc(a_ready, 1)

            def exps_of(t, parity):
                for h in range(2):
                    exp_of(t, parity, h)

            def copy_wd_hi():
                for j in range(2):
                    ks = slice(j * K // 2, (j + 1) * K // 2)
                    act.wait_ge([wd_first_ready, wd_second_ready][j], 1)
                    nc.scalar.activation(wd_hi[:, ks, :], wscale[:, ks, :], ACT.Copy).then_inc(wd_hi_ready, 1)

            def copy_wo(c):
                for h in range(2):
                    if c >= 2:
                        act.wait_ge(setup_filled, filled_by(("p", c - 2, 1)))
                    copy_setup(("wo", c, h), WoT[:, c % 2, h * GH:(h + 1) * GH, :])

            def copy_P_hi(c):
                for h in range(2):
                    copy_setup(("p", c, h), P_hi[:, h * GH:(h + 1) * GH, c * P:(c + 1) * P])

            def copy_a(t, parity):
                for h in range(2):
                    copy_aT_hi(t, parity, h)

            for h in range(2):
                for k in range(K):
                    copy_setup(("wq", h, k),
                               WqT_hi[:, k, h * HALF:(h + 1) * HALF].rearrange("p (g c) -> p g c", g=4))
                    if h == 0 and k == 0:
                        copy_xT_hi(0, 0)
                    if h == 1:
                        if k == 0:
                            act.wait_ge(w_in, 16)
                        nc.scalar.activation(w_f32[:, k, :], w_i8[:, k, :], ACT.Copy).then_inc(w_cast, 1)
            copy_xT_hi(1, 1)
            exps_of(0, 0)
            copy_wd_hi()
            exps_of(1, 1)
            for h in range(2):
                copy_setup(("m", 0, h), MT[:, h * GH:(h + 1) * GH, :])
            copy_xT_hi(2, 0)
            copy_xT_hi(3, 1)
            copy_wo(0)
            make_a(0, 0)
            exp_of(2, 0, 0)
            copy_P_hi(0)
            make_a(1, 1)
            copy_wo(1)
            exp_of(2, 0, 1)
            copy_xT_hi(4, 0)
            copy_P_hi(1)
            exp_of(3, 1, 0)
            copy_wo(2)
            copy_P_hi(2)
            copy_wo(3)
            exp_of(3, 1, 1)
            copy_a(0, 0)
            copy_P_hi(3)
            make_a(2, 0)
            copy_a(1, 1)
            copy_a(2, 0)
            with act.Fori(0, PAIRS) as i:
                for j in range(2):
                    t = AHEAD + 2 * i + j
                    copy_xT_hi(t + 1, 1 - j)
                    exp_of(t, j, 0)
                    make_a(t - 1, 1 - j)
                    exp_of(t, j, 1)
                    copy_a(t - 1, 1 - j)
            for t in range(T - 2, T):
                if t + 1 < T:
                    copy_xT_hi(t + 1, (t + 1) % 2)
                exp_of(t, t % 2, 0)
                make_a(t - 1, (t - 1) % 2)
                exp_of(t, t % 2, 1)
                copy_a(t - 1, (t - 1) % 2)
            make_a(T - 1, (T - 1) % 2)
            copy_a(T - 1, (T - 1) % 2)

        @block.vector
        def _(dve):
            def statistics(t, parity):
                wait_x(dve, t, parity)
                nc.vector.bn_stats(stats[:], tile(t)).then_inc(stats_set, 1)

            def mean_and_variance(t, parity):
                nc.vector.bn_aggr(meanvar[:, parity, :], stats[:]).then_inc(meanvar_ready, 1)

            def variance_eps(t, parity):
                dve.wait_ge(meanvar_ready, t + 1)
                if from_tile(t, 2):
                    dve.wait_ge(rstd_ready, t - 1)
                nc.vector.tensor_scalar_add(vareps[:, parity, :], meanvar[:, parity, 1:2], LN_EPS
                                            ).then_inc(vareps_ready, 1)

            def normalise(t, parity):
                dve.wait_ge(rstd_ready, t + 1)
                if from_tile(t, 1):
                    dve.wait_ge(xT_filled, t)
                nc.vector.tensor_scalar(xn[:], tile(t), meanvar[:, parity, 0:1], rstd[:, parity, :],
                                        ALU.subtract, ALU.mult).then_inc(xn_ready, 1)

            def split_xT_lo(t, parity):
                dve.wait_ge(xT_hi_ready, t + 1)
                if from_tile(t, 2):
                    dve.wait_ge(dense_filled, t - 1)
                nc.vector.tensor_tensor(xT_lo[:, parity, :, :].rearrange("p k r -> p (k r)"), xT_ps[:],
                                        xT_hi[:, parity, :, :].rearrange("p k r -> p (k r)").bitcast(F32),
                                        ALU.subtract).then_inc(xT_lo_ready, 1)

            def setup_lo(what, out, hi):
                dve.wait_ge(setup_copied, filled_by(what))
                nc.vector.tensor_tensor(out, setup_bank(what)[:].rearrange("p (g c) -> p g c", g=4),
                                        hi.bitcast(F32), ALU.subtract).then_inc(setup_lo_ready, 1)

            def add_bias(t, parity, h):
                cols = slice(h * HALF, (h + 1) * HALF)
                if isinstance(t, int) and t == 0 and h == 0:
                    dve.wait_ge(bq_in, 16)
                if h == 0 and from_tile(t, 2):
                    dve.wait_ge(a_ready, t - 1)
                dve.wait_ge(q_filled, 2 * t + h + 1)
                nc.vector.tensor_tensor(tbuf[:, parity, cols], q_ps[h][:],
                                        bq_b[:].rearrange("p g d -> p (g d)")[:, cols], ALU.add
                                        ).then_inc(q_biased, 1)

            def make_s(t, parity, h):
                cols = slice(h * HALF, (h + 1) * HALF)
                dve.wait_ge(exp_ready, 2 * t + h + 1)
                nc.vector.scalar_tensor_tensor(tbuf[:, parity, cols], tbuf[:, parity, cols], 0.0,
                                               ebuf[:, parity, cols], ALU.max, ALU.add).then_inc(s_ready, 1)

            def denominator(t, parity):
                dve.wait_ge(sz_ready, 2 * t + 2)
                nc.vector.reduce_sum(den[:], ebuf[:, parity, :].rearrange("p (g d) -> p g d", g=G), AX.X
                                     ).then_inc(den_ready, 1)
                dve.wait_ge(den_ready, t + 1)
                nc.vector.tensor_scalar_add(den_e[:], den[:], DEN_EPS).then_inc(den_e_ready, 1)
                dve.wait_ge(den_e_ready, t + 1)
                nc.vector.reciprocal(rden[:, parity, :], den_e[:]).then_inc(rden_ready, 1)

            def add_dense(t):
                dve.wait_ge(dense_filled, t + 1)
                nc.vector.tensor_tensor(tile(t), dense_ps[:], tile(t), ALU.add).then_inc(dense_added, 1)

            def split_aT_lo(t, parity, h):
                gs = slice(h * GH, (h + 1) * GH)
                dve.wait_ge(aT_hi_ready, 2 * t + h + 1)
                if from_tile(t, 2):
                    dve.wait_ge(attn_filled, t - 1)
                nc.vector.tensor_tensor(aT_lo[:, parity, gs, :].rearrange("p g r -> p (g r)"), aT_ps[h][:],
                                        aT_hi[:, parity, gs, :].rearrange("p g r -> p (g r)").bitcast(F32),
                                        ALU.subtract).then_inc(aT_lo_ready, 1)

            def add_attn(t, parity):
                dve.wait_ge(attn_filled, t + 1)
                dve.wait_ge(b_added, t + 1)
                nc.vector.tensor_tensor(tile(t), attn_ps[parity][:], tile(t), ALU.add).then_inc(attn_added, 1)

            def sum_wo(c):
                for q in (1, 3):
                    k = 4 * c + q
                    n = k + 4
                    v = stage(n % SLOTS).rearrange("p (g u v d) -> p g u v d", g=2, u=2, v=2)
                    if c >= 2 and q == 1:
                        dve.wait_ge(setup_filled, filled_by(("wo", c - 2, 1)))
                    dve.wait_ge(stage_in[n % SLOTS], 16 * (n // SLOTS + 1))
                    nc.vector.tensor_tensor(v[:, :, :, 0, :], v[:, :, :, 0, :], v[:, :, :, 1, :], ALU.add
                                            ).then_inc(dve_pairs, 1)
                    dve.wait_ge(dve_pairs, k // 2 + 1)
                    nc.vector.tensor_tensor(Wo_sum[:, c % 2, 2 * q:2 * q + 2, :], v[:, :, 0, 0, :],
                                            v[:, :, 1, 0, :], ALU.add).then_inc(dve_summed, 1)

            def P_split(c):
                for h in range(2):
                    gs, ns = slice(h * GH, (h + 1) * GH), slice(c * P, (c + 1) * P)
                    setup_lo(("p", c, h), P_lo[:, gs, ns], P_hi[:, gs, ns])

            def statistics_at_once(t):
                statistics(t, t % 2)
                dve.wait_ge(stats_set, t + 1)
                mean_and_variance(t, t % 2)
                variance_eps(t, t % 2)

            def split_wq_lo(h, k):
                cs = slice(h * HALF, (h + 1) * HALF)
                setup_lo(("wq", h, k), WqT_lo[:, k, cs].rearrange("p (g c) -> p g c", g=4),
                         WqT_hi[:, k, cs].rearrange("p (g c) -> p g c", g=4))

            def scale_w():
                dve.wait_ge(wscale_in, 16)
                dve.wait_ge(w_cast, K)
                nc.vector.tensor_tensor(wscale[:, K // 2:, :], w_f32[:, K // 2:, :], wscale[:, K // 2:, :], ALU.mult
                                        ).then_inc(wd_second_ready, 1)

            def split_wd_lo(j):
                ks = slice(j * K // 2, (j + 1) * K // 2)
                dve.wait_ge(wd_hi_ready, j + 1)
                nc.vector.tensor_tensor(wd_lo[:, ks, :], wscale[:, ks, :], wd_hi[:, ks, :].bitcast(F32),
                                        ALU.subtract).then_inc(wd_lo_ready, 1)

            def make_s_both(t, parity):
                for h in range(2):
                    make_s(t, parity, h)

            def split_a(t, parity):
                for h in range(2):
                    split_aT_lo(t, parity, h)

            def q_step(t, parity, stats_ahead=True, next_x=True):
                if stats_ahead:
                    statistics(t + 2, parity)
                    dve.wait_ge(stats_set, t + 3)
                add_bias(t, parity, 0)
                if stats_ahead:
                    mean_and_variance(t + 2, parity)
                    variance_eps(t + 2, parity)
                denominator(t - 1, 1 - parity)
                if next_x:
                    split_xT_lo(t + 1, 1 - parity)
                add_bias(t, parity, 1)
                if stats_ahead:
                    normalise(t + 2, parity)
                make_s_both(t, parity)
                add_dense(t)

            nc.vector.memset(warm, 0.0).then_inc(warm_set, 1)
            statistics_at_once(0)
            normalise(0, 0)
            split_wq_lo(0, 0)
            split_xT_lo(0, 0)
            for k in range(1, K):
                split_wq_lo(0, k)
            statistics_at_once(1)
            split_wq_lo(1, 0)
            normalise(1, 1)
            for k in range(1, K):
                split_wq_lo(1, k)
            add_bias(0, 0, 0)
            split_xT_lo(1, 1)
            add_bias(0, 0, 1)
            scale_w()
            statistics_at_once(2)
            split_wd_lo(0)
            add_bias(1, 1, 0)
            split_wd_lo(1)
            add_bias(1, 1, 1)
            normalise(2, 0)
            make_s(0, 0, 0)
            add_dense(0)
            make_s(0, 0, 1)
            statistics_at_once(3)
            split_xT_lo(2, 0)
            normalise(3, 1)
            sum_wo(0)
            make_s_both(1, 1)
            denominator(0, 0)
            add_dense(1)
            sum_wo(1)
            statistics_at_once(4)
            add_bias(2, 0, 0)
            denominator(1, 1)
            split_xT_lo(3, 1)
            add_bias(2, 0, 1)
            normalise(4, 0)
            make_s(2, 0, 0)
            P_split(0)
            sum_wo(2)
            make_s(2, 0, 1)
            add_dense(2)
            add_bias(3, 1, 0)
            P_split(1)
            sum_wo(3)
            split_xT_lo(4, 0)
            add_bias(3, 1, 1)
            statistics_at_once(5)
            denominator(2, 0)
            normalise(5, 1)
            P_split(2)
            split_a(0, 0)
            P_split(3)
            make_s_both(3, 1)
            add_dense(3)
            split_a(1, 1)
            add_attn(0, 0)
            split_a(2, 0)
            add_attn(1, 1)
            with dve.Fori(0, PAIRS) as i:
                for j in range(2):
                    t = AHEAD + 2 * i + j
                    q_step(t, j)
                    add_attn(t - 2, j)
                    split_a(t - 1, 1 - j)
            for t in range(T - 2, T):
                q_step(t, t % 2, stats_ahead=False, next_x=t + 1 < T)
                if t == T - 1:
                    split_a(t - 1, (t - 1) % 2)
                    denominator(t, t % 2)
                add_attn(t - 2, t % 2)
                if t < T - 1:
                    split_a(t - 1, (t - 1) % 2)
            split_a(T - 1, (T - 1) % 2)
            add_attn(T - 2, T % 2)
            for c in range(2):
                cols = slice(c * HID // 2, (c + 1) * HID // 2)
                dve.wait_ge(attn_filled, T + c)
                dve.wait_ge(b_added, T)
                nc.vector.tensor_tensor(x[:, T - 1, cols], last_attn_ps(c), x[:, T - 1, cols], ALU.add
                                        ).then_inc(attn_added, 1)

        @block.tensor
        def _(pe):
            def transpose_x(t):
                pe.wait_ge(xn_ready, t + 1)
                if from_tile(t, 1):
                    pe.wait_ge(xT_lo_ready, t)
                for k in range(K):
                    last = nc.tensor.transpose(xT_ps[:, k * P:(k + 1) * P], xn[:, k * P:(k + 1) * P], ident[:])
                last.then_inc(xT_filled, 1)

            def three_passes(out, x_hi, x_lo, w_hi, w_lo, start, stop):
                nc.tensor.matmul(out, x_hi, w_hi, start=start, stop=False)
                nc.tensor.matmul(out, x_hi, w_lo, start=False, stop=False)
                return nc.tensor.matmul(out, x_lo, w_hi, start=False, stop=stop)

            def q_chunk(parity, h, k):
                cols = slice(h * HALF, (h + 1) * HALF)
                return three_passes(q_ps[h][:], xT_hi[:, parity, k, :], xT_lo[:, parity, k, :],
                                    WqT_hi[:, k, cols], WqT_lo[:, k, cols], k == 0, k == K - 1)

            def product_q(t, parity, h):
                pe.wait_ge(xT_lo_ready, t + 1)
                if from_tile(t, 1):
                    pe.wait_ge(q_biased, 2 * t - 1 + h)
                for k in range(K):
                    last = q_chunk(parity, h, k)
                last.then_inc(q_filled, 1)

            def product_dense(t, parity):
                if from_tile(t, 1):
                    pe.wait_ge(dense_added, t)
                for k in range(K):
                    if isinstance(t, int) and t == 0:
                        pe.wait_ge(wd_lo_ready, 2 * k // K + 1)
                    last = three_passes(dense_ps[:], xT_hi[:, parity, k, :], xT_lo[:, parity, k, :],
                                        wd_hi[:, k, :], wd_lo[:, k, :], k == 0, k == K - 1)
                last.then_inc(dense_filled, 1)

            def transpose_a(t, parity):
                pe.wait_ge(a_ready, t + 1)
                if isinstance(t, int) and t == 0:
                    pe.wait_ge(setup_copied, filled_by(("wo", NC - 1, 1)))
                for h in range(2):
                    if from_tile(t, 1):
                        pe.wait_ge(aT_lo_ready, 2 * t - 1 + h)
                    for i in range(GH):
                        g = h * GH + i
                        last = nc.tensor.transpose(aT_ps[h][:, i * P:(i + 1) * P],
                                                   a[:, a_slot(t, parity), g * D:(g + 1) * D], ident[:])
                    last.then_inc(aT_filled, 1)

            def product_attn(t, parity, between=None):
                if from_tile(t, 2):
                    pe.wait_ge(attn_added, t - 1)
                for g in range(G):
                    if g == GH and between is not None:
                        between()
                    if g % GH == 0:
                        h = g // GH
                        pe.wait_ge(aT_lo_ready, 2 * t + h + 1)
                        if isinstance(t, int) and t == 0:
                            pe.wait_ge(setup_lo_ready, lo_by(("p", NC - 1, h)))
                    last = three_passes(attn_ps[parity][:], aT_hi[:, parity, g, :], aT_lo[:, parity, g, :],
                                        P_hi[:, g, :], P_lo[:, g, :], g == 0, g == G - 1)
                last.then_inc(attn_filled, 1)

            def setup_free(what):
                before = [v for v in SETUP[:USE[what]] if setup_bank(v) is setup_bank(what)]
                if what[:2] == ("p", NC - 1):
                    pe.wait_ge(q_biased, 2 * AHEAD)
                elif before and before[-1][0] in ("wq", "p"):
                    pe.wait_ge(setup_lo_ready, lo_by(before[-1]))
                elif before:
                    pe.wait_ge(setup_copied, filled_by(before[-1]))

            def transposes(what, blocks):
                setup_free(what)
                for i, block_in in enumerate(blocks):
                    last = nc.tensor.transpose(setup_bank(what)[:, i * P:(i + 1) * P], block_in, ident[:])
                last.then_inc(setup_filled, 1)

            def transpose_wq(h, k):
                i, k_in = 2 * h + 2 * k // K, k % (K // 2)
                if k_in == 0:
                    pe.wait_ge(stage_in[i], 16)
                piece = stage(i).rearrange("p (g c) -> p g c", g=GH)
                transposes(("wq", h, k), [piece[:, g, k_in * P:(k_in + 1) * P] for g in range(GH)])

            def transpose_m():
                pe.wait_ge(M_in, 16)
                for h in range(2):
                    transposes(("m", 0, h), [M_sb[:, h * GH + i, :] for i in range(GH)])

            def transpose_wo(c):
                pe.wait_ge(pool_summed, 2 * c + 2)
                pe.wait_ge(dve_summed, 2 * c + 2)
                for h in range(2):
                    transposes(("wo", c, h), [Wo_sum[:, c % 2, h * GH + i, :] for i in range(GH)])

            def product_P(c):
                for h in range(2):
                    pe.wait_ge(setup_copied, filled_by(("wo", c, h)))
                    setup_free(("p", c, h))
                    for i in range(GH):
                        g = h * GH + i
                        last = nc.tensor.matmul(setup_bank(("p", c, h))[:, i * P:(i + 1) * P], MT[:, g, :],
                                                WoT[:, c % 2, g, :], start=True, stop=True)
                    last.then_inc(setup_filled, 1)

            pe.wait_ge(warm_set, 1)
            for _ in range(WARM_UP):
                nc.tensor.matmul(xT_ps[:, 0:P], warm, warm, start=True, stop=True)
            pe.wait_ge(consts_set, 3)
            transpose_wq(0, 0)
            transpose_x(0)
            for k in range(1, K):
                transpose_wq(0, k)
            pe.wait_ge(xT_lo_ready, 1)
            for h in range(2):
                for k in range(K):
                    pe.wait_ge(setup_lo_ready, lo_by(("wq", h, k)))
                    if h == 1 and k == 0:
                        pe.wait_ge(setup_lo_ready, lo_by(("wq", 1, 1)))
                    last = q_chunk(0, h, k)
                    if k == K - 1:
                        last.then_inc(q_filled, 1)
                    if h == 0:
                        transpose_wq(1, k)
                    if h == 0 and k == K - 1:
                        transpose_x(1)
            for h in range(2):
                product_q(1, 1, h)
            product_dense(0, 0)
            transpose_m()
            transpose_x(2)
            product_dense(1, 1)
            product_q(2, 0, 0)
            transpose_x(3)
            transpose_wo(0)
            product_q(2, 0, 1)
            product_P(0)
            product_dense(2, 0)
            transpose_wo(1)
            product_q(3, 1, 0)
            transpose_x(4)
            product_P(1)
            transpose_wo(2)
            product_q(3, 1, 1)
            product_P(2)
            transpose_wo(3)
            product_dense(3, 1)
            transpose_a(0, 0)
            product_P(3)
            transpose_a(1, 1)
            product_attn(0, 0)
            transpose_a(2, 0)
            product_attn(1, 1)
            with pe.Fori(0, PAIRS) as i:
                for j in range(2):
                    t = AHEAD + 2 * i + j
                    product_q(t, j, 0)
                    transpose_x(t + 1)
                    product_q(t, j, 1)
                    product_dense(t, j)
                    product_attn(t - 2, j)
                    transpose_a(t - 1, 1 - j)
            for t in range(T - 2, T):
                product_q(t, t % 2, 0)
                if t + 1 < T:
                    transpose_x(t + 1)
                product_q(t, t % 2, 1)
                product_dense(t, t % 2)
                if t == T - 1:
                    transpose_a(t - 1, (t - 1) % 2)
                product_attn(t - 2, t % 2)
                if t < T - 1:
                    transpose_a(t - 1, (t - 1) % 2)
            product_attn(T - 2, T % 2, between=lambda: transpose_a(T - 1, (T - 1) % 2))
            for c in range(2):
                cols = slice(c * HID // 2, (c + 1) * HID // 2)
                for g in range(G):
                    if c == 0 and g % GH == 0:
                        pe.wait_ge(aT_lo_ready, 2 * (T - 1) + g // GH + 1)
                    last = three_passes(last_attn_ps(c), aT_hi[:, (T - 1) % 2, g, :], aT_lo[:, (T - 1) % 2, g, :],
                                        P_hi[:, g, cols], P_lo[:, g, cols], g == 0, g == G - 1)
                last.then_inc(attn_filled, 1)


_INS = ["L0_attn_hidden_states", "L0_attn_Wq", "L0_attn_bq", "L0_attn_Wo", "L0_attn_M", "L0_attn_z",
        "L0_ffn_w", "L0_ffn_w_scale", "L0_ffn_b"]


def kernel(**inputs):
    import numpy as np
    import concourse.bacc as bacc
    from concourse.bass_utils import run_bass_kernel_spmd

    nc = bacc.Bacc("TRN2", target_bir_lowering=False, num_devices=1)
    arrays, args = {}, []
    for name in _INS:
        v = np.ascontiguousarray(inputs[name])
        if v.dtype == np.int8:
            v = v.view(np.int32)
        arrays[f"in_{name}"] = v
        args.append(nc.dram_tensor(f"in_{name}", v.shape, mybir.dt.from_np(v.dtype), kind="ExternalInput").ap())
    shape = inputs["L0_attn_hidden_states"].shape
    out = nc.dram_tensor("out", shape, F32, kind="ExternalOutput").ap()
    retrieval_and_dense(nc, *args, out)
    result = run_bass_kernel_spmd(nc, [arrays], core_ids=[0])
    return result.results[0]["out"]
```
